# Optimizing a Trainium2 kernel written in Bass

```python
import numpy as np
import jax
import jax.numpy as jnp

def _softmax(x, axis=-1):
    return jax.nn.softmax(x, axis=axis)

def _gelu(x):
    return jax.nn.gelu(x, approximate=True)

def _silu(x):
    return jax.nn.silu(x)

def _sigmoid(x):
    return jax.nn.sigmoid(x)

def _layernorm(x, axis=-1, eps=1e-05):
    m = jnp.mean(x, axis=axis, keepdims=True)
    v = jnp.var(x, axis=axis, keepdims=True)
    return (x - m) / jnp.sqrt(v + eps)

def _scatter_add(tgt, idx, src, axis=0):
    return tgt.at[idx].add(src)

def _segment_sum(src, seg, n):
    return jax.ops.segment_sum(src, seg, n)
kernel_name = 'mk_xattn_ffn_d1_seqx_r8_4cc2b4'

def setup_inputs(seed: int=0):
    np.random.seed(seed)
    _w = jnp.asarray

    def _rec_inputs():
        import jax
        import jax.numpy as jnp
        _rk = jax.random.key(seed)
        x = -0.0002928 + 1 * jax.random.normal(jax.random.fold_in(_rk, 1), (64, 128, 128), jnp.float32)
        _lenS = 128 - jax.random.randint(jax.random.fold_in(_rk, 7), (64,), 0, max(1, 128 // 4) + 1, jnp.int32)
        _lenS2 = 77 - jax.random.randint(jax.random.fold_in(_rk, 8), (64,), 0, max(1, 77 // 4) + 1, jnp.int32)
        _ctx_1024P = jax.random.normal(jax.random.fold_in(_rk, 11), (64, 16, 128), jnp.float32)
        _ctx_1024c = jax.random.dirichlet(jax.random.fold_in(_rk, 511), 0.3 * jnp.ones((16,), jnp.float32), (64, 77))
        _ctx_1024t = jnp.einsum('bsk,bkd->bsd', _ctx_1024c, _ctx_1024P)
        _ctx_1024t = _ctx_1024t * jax.lax.rsqrt(jnp.mean(jnp.square(_ctx_1024t)) + 1e-12) * 0.953939
        ctx_1024 = -1.39393e-06 + 0.999914 * (_ctx_1024t + 0.3 * jax.random.normal(jax.random.fold_in(_rk, 611), (64, 77, 128), jnp.float32))
        return (x, ctx_1024)
    x, ctx_1024 = _rec_inputs()

    def _L0_xattn_setup():
        import jax, jax.numpy as jnp
        import numpy as np
        key = jax.random.key(seed)
        ks = jax.random.split(key, 8)
        B, T, S = (32, 128, 128)
        Din, H, C = (128, 128, 128)
        s = 0.02
        return {'x': jax.random.normal(ks[0], (B, T, Din), jnp.float32), 'context': jax.random.normal(ks[1], (B, S, C), jnp.float32), 'W_ih': jax.random.normal(ks[2], (4 * H, Din + H), jnp.float32) * s, 'W_hh': jax.random.normal(ks[3], (4 * H, H), jnp.float32) * s, 'b_ih': jnp.zeros((4 * H,), jnp.float32), 'b_hh': jnp.zeros((4 * H,), jnp.float32), 'Wq': jax.random.normal(ks[4], (C, H), jnp.float32) * s, 'Wout': jax.random.normal(ks[5], (H, C + H), jnp.float32) * s, 'b_out': jnp.zeros((H,), jnp.float32)}
    _L0_xattn_all = _L0_xattn_setup()
    _L0_xattn_in = {k: v for k, v in _L0_xattn_all.items() if k in ('W_ih', 'W_hh', 'b_ih', 'b_hh', 'Wq', 'Wout', 'b_out')}
    del _L0_xattn_all

    def _L0_ffn_setup():
        import jax, jax.numpy as jnp
        import numpy as np
        NEG_INF = -1e+30
        K = 2
        key = jax.random.key(seed)
        ks = jax.random.split(key, 5)
        B, S, D, O, E = (8, 256, 128, 128, 8)
        scale = 1.0 / np.sqrt(D)
        return {'x': jax.random.normal(ks[0], (B, S, D), dtype=jnp.float32), 'gate_w': jax.random.normal(ks[1], (E, D), dtype=jnp.float32) * scale, 'gate_b': jnp.zeros((E,), dtype=jnp.float32), 'expert_w': jax.random.normal(ks[2], (E, O, D), dtype=jnp.float32) * scale, 'expert_b': jnp.zeros((E, O), dtype=jnp.float32)}
    _L0_ffn_all = _L0_ffn_setup()
    _L0_ffn_in = {k: v for k, v in _L0_ffn_all.items() if k in ('gate_w', 'gate_b', 'expert_w', 'expert_b')}
    del _L0_ffn_all
    return {'x': x, 'ctx_1024': ctx_1024, 'L0_xattn_W_ih': _L0_xattn_in['W_ih'], 'L0_xattn_W_hh': _L0_xattn_in['W_hh'], 'L0_xattn_b_ih': _L0_xattn_in['b_ih'], 'L0_xattn_b_hh': _L0_xattn_in['b_hh'], 'L0_xattn_Wq': _L0_xattn_in['Wq'], 'L0_xattn_Wout': _L0_xattn_in['Wout'], 'L0_xattn_b_out': _L0_xattn_in['b_out'], 'L0_ffn_gate_w': _L0_ffn_in['gate_w'], 'L0_ffn_gate_b': _L0_ffn_in['gate_b'], 'L0_ffn_expert_w': _L0_ffn_in['expert_w'], 'L0_ffn_expert_b': _L0_ffn_in['expert_b']}

def reference(x, ctx_1024, L0_xattn_W_ih, L0_xattn_W_hh, L0_xattn_b_ih, L0_xattn_b_hh, L0_xattn_Wq, L0_xattn_Wout, L0_xattn_b_out, L0_ffn_gate_w, L0_ffn_gate_b, L0_ffn_expert_w, L0_ffn_expert_b):
    import jax
    import jax.numpy as jnp

    def _L0_xattn_ref(x, context, W_ih, W_hh, b_ih, b_hh, Wq, Wout, b_out):
        import jax, jax.numpy as jnp
        import numpy as np
        B, T, Din = x.shape
        H = W_hh.shape[1]

        def attend(h):
            q = h @ Wq.T
            scores = jnp.einsum('bc,bsc->bs', q, context)
            alpha = jax.nn.softmax(scores, axis=-1)
            ctx = jnp.einsum('bs,bsc->bc', alpha, context)
            return jnp.tanh(jnp.concatenate([ctx, h], axis=-1) @ Wout.T + b_out)

        def step(carry, x_t):
            h, c, attn = carry
            inp = jnp.concatenate([x_t, attn], axis=-1)
            gates = inp @ W_ih.T + b_ih + h @ W_hh.T + b_hh
            i, f, g, o = jnp.split(gates, 4, axis=-1)
            c = jax.nn.sigmoid(f) * c + jax.nn.sigmoid(i) * jnp.tanh(g)
            h = jax.nn.sigmoid(o) * jnp.tanh(c)
            out = attn_out = attend(h)
            return ((h, c, attn_out), out)
        h0 = jnp.zeros((B, H), x.dtype)
        init = (h0, h0, h0)
        xs = jnp.swapaxes(x, 0, 1)
        _, outs = jax.lax.scan(step, init, xs)
        return jnp.swapaxes(outs, 0, 1)

    def _L0_ffn_ref(x, gate_w, gate_b, expert_w, expert_b):
        import jax, jax.numpy as jnp
        import numpy as np
        NEG_INF = -1e+30
        K = 2
        pooled = x.mean(axis=1)
        logits = pooled @ gate_w.T + gate_b
        topk_vals, _ = jax.lax.top_k(logits, K)
        min_topk = topk_vals[:, -1:]
        masked = jnp.where(logits < min_topk, -jnp.inf, logits)
        gates = jax.nn.softmax(masked, axis=-1)
        expert_out = jax.nn.gelu(jnp.einsum('bsd,eod->beso', x, expert_w) + expert_b[None, :, None, :], approximate=False)
        return jnp.einsum('be,beso->bso', gates, expert_out)
    x = x + _L0_xattn_ref(_layernorm(x, axis=-1), ctx_1024, L0_xattn_W_ih, L0_xattn_W_hh, L0_xattn_b_ih, L0_xattn_b_hh, L0_xattn_Wq, L0_xattn_Wout, L0_xattn_b_out)
    x = x + _L0_ffn_ref(_layernorm(x, axis=-1), L0_ffn_gate_w, L0_ffn_gate_b, L0_ffn_expert_w, L0_ffn_expert_b)
    return x

_drawn_inputs = setup_inputs


def setup_inputs(seed=0):
    import zlib

    import numpy as np

    out = dict(_drawn_inputs(seed))
    spreads = {'L0_xattn_b_ih': (0.0, 0.1),
     'L0_xattn_b_hh': (0.0, 0.1),
     'L0_xattn_b_out': (0.0, 0.1),
     'L0_ffn_gate_b': (0.0, 0.1),
     'L0_ffn_expert_b': (0.0, 0.1)}
    factors = {}
    for name, (base, spread) in spreads.items():
        noise = np.random.default_rng([zlib.crc32(name.encode()), seed]).standard_normal(out[name].shape)
        drawn = base * np.exp(spread * noise) if base else spread * noise
        out[name] = jnp.asarray(drawn.astype(out[name].dtype))
    for name, factor in factors.items():
        out[name] = (out[name] * factor).astype(out[name].dtype)
    return out
```

```python
from contextlib import ExitStack

import numpy as np

import concourse.bass as bass
from concourse import mybir

ALU = mybir.AluOpType
ACT = mybir.ActivationFunctionType
AX_X = mybir.AxisListType.X
F32 = mybir.dt.float32
BF16 = mybir.dt.bfloat16

B, T, D, S, E = 64, 128, 128, 77, 8
H = D
EPS = 1e-5
G = 2
NB = B // G
U = 2
PAIRS = T // U
TURNS = U * G
Q = 3
SA = 64
SB = S - SA
SD = SA + Q * SB
PRODUCTS = ((2, 0), (1, 1), (0, 2), (1, 0), (0, 1), (0, 0))
KG = 4
KSTEPS = B // KG
FG = 4
FTILES = B // FG

C_ID = 0
C_SEL = C_ID + 128
C_FOLD = C_SEL + 2 * SD
C_MASK = C_FOLD + B
C_ALL = C_MASK + 5


def constants():
    c = np.zeros((128, C_ALL), np.float32)
    c[:, C_ID:C_ID + 128] = np.eye(128)
    for col in range(Q * S):
        pack, row, s = col // 128, col % 128, col % S
        for n in range(SD):
            if (n if n < S else SA + (n - S) % SB) == s:
                c[row, C_SEL + pack * SD + n] = 1
    for r in range(128):
        c[r, C_FOLD + r % B] = 1.0 / T
    c[SA:, C_MASK + 0] = -1
    c[:SA, C_MASK + 1] = -1
    c[SA + SB:, C_MASK + 1] = -1
    c[:SA, C_MASK + 2] = -1
    c[SA + 2 * SB:, C_MASK + 2] = -1
    c[32:, C_MASK + 3] = -1
    c[64:, C_MASK + 4] = -1
    return c


def xattn_moe(nc, x_tbd, ctx_dup, w_gates, b_ih, b_hh, w_q, w_out, b_out,
              gate_w, gate_b, expert_w, expert_b, consts, out):
    x_tb = x_tbd.rearrange("t b d -> (t b) d")
    with ExitStack() as ctx:
        def sb(name, shape, dt):
            return ctx.enter_context(nc.sbuf_tensor(name, shape, dt))

        def sem(name):
            return ctx.enter_context(nc.semaphore(name))

        cst = sb("cst", [128, C_ALL], F32)
        ident = cst[:, C_ID:C_ID + 128]
        fold = cst[:, C_FOLD:C_FOLD + B]

        def sel(pack):
            return cst[:, C_SEL + pack * SD:C_SEL + (pack + 1) * SD]

        def mask(n):
            return cst[:, C_MASK + n:C_MASK + n + 1]

        ctx_attn = sb("ctx_attn", [128, B, 128], F32)
        kst = sb("kst", [128, B, 2 * 128], BF16)
        vst = sb("vst", [128, B, 2, 128], BF16)
        zT = sb("zT", [128, B, T], F32)
        wf = sb("wf", [128, 13, 128], F32)
        w3 = sb("w3", [128, Q, 13, 128], BF16)
        wq = sb("wq", [128, H], F32)
        wo = sb("wo", [128, 128], F32)
        bi = sb("bi", [128, 4, 128], F32)
        bh = sb("bh", [128, 4, 128], F32)
        bhi = sb("bhi", [128, 4, 128], BF16)
        b3 = sb("b3", [128, 4, 128], BF16)
        ones = sb("ones", [128, B], BF16)
        onesf = sb("onesf", [B, 128], F32)
        bo = sb("bo", [128, 1], F32)
        ew = sb("ew", [128, E, 128], F32)
        eb = sb("eb", [128, E], F32)
        gw = sb("gw", [128, E], F32)
        gb = sb("gb", [B, E], F32)
        kr = sb("kr", [128, 2, KG, S], F32)
        v0hi = sb("v0hi", [128, 2, KG, 128], BF16)
        v1hi = sb("v1hi", [128, 2, KG, 128], BF16)
        v1r = sb("v1r", [128, 2, KG, 128], F32)
        v1mid = sb("v1mid", [128, 2, KG, 128], BF16)
        tg = [sb(f"tg{g}", [128, 4, NB], F32) for g in range(G)]
        c2 = [sb(f"c2_{g}", [128, NB], F32) for g in range(G)]
        in_term = [sb(f"in_term{g}", [128, NB], F32) for g in range(G)]
        forget_term = [sb(f"forget_term{g}", [128, NB], F32) for g in range(G)]
        tc = [sb(f"tc{g}", [128, NB], F32) for g in range(G)]
        h2 = [sb(f"h2_{g}", [128, NB], F32) for g in range(G)]
        hr = [sb(f"hr{g}", [128, NB], F32) for g in range(G)]
        hq = [sb(f"hq{g}", [128, Q, NB], BF16) for g in range(G)]
        sc = [sb(f"sc{g}", [128, 2, NB], F32) for g in range(G)]
        neg_max = [sb(f"neg_max{g}", [NB, 1], F32) for g in range(G)]
        expo = [sb(f"expo{g}", [NB, SD], F32) for g in range(G)]
        den = [sb(f"den{g}", [NB, 1], F32) for g in range(G)]
        rden = [sb(f"rden{g}", [NB, 1], F32) for g in range(G)]
        alpha = [sb(f"alpha{g}", [NB, 2, 128], F32) for g in range(G)]
        ar = [sb(f"ar{g}", [128, 2, NB], F32) for g in range(G)]
        aq = [sb(f"aq{g}", [128, Q, 2, NB], BF16) for g in range(G)]
        at_in = [sb(f"at_in{g}", [128, NB], F32) for g in range(G)]
        at_r = [sb(f"at_r{g}", [128, NB], F32) for g in range(G)]
        atq = [sb(f"atq{g}", [128, Q, NB], BF16) for g in range(G)]
        at = sb("at", [128, U, B], F32)
        xa = sb("xa", [128, D], F32)
        xb = sb("xb", [128, D], F32)
        st1 = sb("st1", [128, 6], F32)
        st2 = sb("st2", [128, 6], F32)
        mv1 = sb("mv1", [128, 2], F32)
        mv2 = sb("mv2", [128, 2], F32)
        ve1 = sb("ve1", [128, 1], F32)
        ve2 = sb("ve2", [128, 1], F32)
        rs1 = sb("rs1", [128, 1], F32)
        rs2 = sb("rs2", [128, 1], F32)
        mhalf = sb("mhalf", [128, 1], F32)
        xn = sb("xn", [128, D], F32)
        xq = sb("xq", [128, Q, U * B], BF16)
        xr = sb("xr", [128, U * B], F32)
        y = sb("y", [128, D], F32)
        z = sb("z", [128, D], F32)
        zsum = sb("zsum", [128, D], F32)
        pooled = sb("pooled", [128, B], F32)
        lg = sb("lg", [B, E], F32)
        top = sb("top", [B, 8], F32)
        ntop = sb("ntop", [B, 1], F32)
        keep = sb("keep", [B, E], F32)
        ge = sb("ge", [B, E], F32)
        gk = sb("gk", [B, E], F32)
        gs = sb("gs", [B, 1], F32)
        gr = sb("gr", [B, 1], F32)
        gd = sb("gd", [B, B, E], F32)
        gates = sb("gates", [128, B, E], F32)
        gl = sb("gl", [128, 4, FG, T], F32)
        acc = sb("acc", [128, 2, FG, T], F32)
        xo = v1r
        res = sb("res", [128, 2, FG, D], F32)

        bank = [ctx.enter_context(nc.psum_tensor(f"bank{n}", [128, 512], F32)) for n in range(8)]
        ps_gates = [bank[g][:, 0:4 * NB].rearrange("p (m b) -> p m b", m=4) for g in range(G)]
        ps_val = [bank[g][:, 4 * NB:(4 + Q) * NB].rearrange("p (b q) -> p b q", q=Q) for g in range(G)]
        ps_sc = [bank[2 + g][:, 0:2 * NB * Q].rearrange("p (k b q) -> p k b q", k=2, q=Q) for g in range(G)]
        ps_row = [bank[2 + g][0:NB, 256:256 + SD] for g in range(G)]
        ps_alT = [bank[2 + g][:, 384:384 + 2 * NB].rearrange("p (k b) -> p k b", k=2) for g in range(G)]
        ps_xT = bank[4][:, 0:128]
        ps_y = bank[5][:, 0:128]
        ps_zT = bank[6][:, 0:128]

        s_w = sem("weights_loaded")
        s_ctx = [sem(f"context_loaded{n}") for n in range(4)]
        s_ew = sem("expert_weights_loaded")
        s_ms = sem("memsets_done")
        s_pm = sem("pool_memsets_done")
        s_kc = sem("kst_cleared")
        s_ws = sem("weights_scaled")
        s_wh = sem("weights_hi")
        s_wr = sem("weights_rest")
        s_wm = sem("weights_mid")
        s_wl = sem("weights_split")
        s_b = sem("bias_chain")
        s_kvp = sem("kv_products")
        s_kvh = sem("kv_hi")
        s_kvr = sem("kv_rest")
        s_kvm = sem("kv_mid")
        s_kl = sem("k_lo")
        s_vl = sem("v_lo")
        s_gates = sem("gates_ready")
        s_tg = sem("gates_tanh")
        s_ct = sem("c_terms")
        s_c = sem("c_ready")
        s_tc = sem("c_tanh")
        s_h = sem("h_hi")
        s_hm = sem("h_mid")
        s_hl = sem("h_split")
        s_sp = sem("score_parts")
        s_ss = sem("score_sums")
        s_row = sem("score_rows")
        s_mx = sem("neg_max_ready")
        s_ex = sem("exp_ready")
        s_rd = sem("rden_ready")
        s_al = sem("alpha_ready")
        s_aT = sem("alpha_transposed")
        s_ah = sem("alpha_hi")
        s_am = sem("alpha_mid")
        s_as = sem("alpha_split")
        s_vp = sem("value_parts")
        s_vs = sem("value_sums")
        s_at = sem("attn_ready")
        s_tm = sem("attn_mid")
        s_ts = sem("attn_split")
        s_xa = sem("xa_loaded")
        s_x1 = sem("ln1_stats")
        s_x2 = sem("ln1_mean_var")
        s_xv = sem("ln1_var_eps")
        s_xs = sem("ln1_rstd")
        s_xn = sem("ln1_ready")
        s_xT = sem("ln1_transposed")
        s_xh = sem("x_hi")
        s_xm = sem("x_mid")
        s_xl = sem("x_split")
        s_xg = sem("x_gates_done")
        s_xb = sem("xb_loaded")
        s_yT = sem("attn_pair_transposed")
        s_sv = sem("attn_pair_saved")
        s_y = sem("y_ready")
        s_y1 = sem("ln2_stats")
        s_y2 = sem("ln2_mean_var")
        s_yv = sem("ln2_var_eps")
        s_ys = sem("ln2_rstd")
        s_z = sem("z_ready")
        s_zs = sem("z_summed")
        s_zT = sem("z_transposed")
        s_zc = sem("z_stored")
        s_gt = sem("gating_tensor")
        s_gv = sem("gating_vector")
        s_ga = sem("gating_scalar")
        s_fp = sem("expert_products")
        s_fg = sem("expert_gelu")
        s_fa = sem("expert_added")
        s_fT = sem("tile_transposed")
        s_fr = sem("tile_result")
        s_xo = [sem(f"residual_loaded{n}") for n in range(2)]
        s_held = sem("held")
        s_out = [sem(f"tile_stored{n}") for n in range(2)]

        block = ctx.enter_context(nc.Block())

        class Counts:

            def __init__(self, eng, i):
                self.eng, self.i, self.known = eng, i, {}

            def at_least(self, s, per_pair, n):
                if isinstance(self.i, int):
                    if per_pair * self.i + n > 0:
                        self.eng.wait_ge(s, per_pair * self.i + n)
                    return
                if (per_pair, n) not in self.known:
                    self.known[per_pair, n] = self.eng.snap(self.i * per_pair + n)
                self.eng.wait_ge(s, self.known[per_pair, n])

            def hold(self):
                if not isinstance(self.i, int):
                    self.eng.sem_inc(s_held, 1)

            def turn(self, s, k):
                self.at_least(s, TURNS, k + 1)

            def step(self, s, k):
                self.at_least(s, U, k + 1)

            def pair(self, s, k, by=1):
                self.at_least(s, by, by * (k + 1))

        def run_pairs(eng, body):
            body(Counts(eng, 0), True, False)
            with eng.Fori(1, PAIRS - 1) as i:
                body(Counts(eng, i), False, False)
            body(Counts(eng, PAIRS - 1), False, True)

        def run_tiles(eng, body):
            body(Counts(eng, 0), True, False)
            with eng.Fori(1, FTILES // 2 - 1) as i:
                body(Counts(eng, i), False, False)
            body(Counts(eng, FTILES // 2 - 1), False, True)

        @block.sync
        def _(sp):
            sp.dma_start(cst[:, :], consts).then_inc(s_w, 16)
            sp.dma_start(wo[:, :], w_out).then_inc(s_w, 16)
            sp.dma_start(wq[:, :], w_q).then_inc(s_w, 16)
            for n in range(4):
                part = slice(n * B // 4, (n + 1) * B // 4)
                sp.dma_start(ctx_attn[:, part, :], ctx_dup[:, part, :]).then_inc(s_ctx[n], 16)
            sp.dma_start(xb[:, :], x_tb[0:128, :]).then_inc(s_xb, 16)
            sp.dma_start(ew[:, :, :], expert_w).then_inc(s_ew, 16)
            sp.dma_start(eb[:, :], expert_b).then_inc(s_ew, 16)
            sp.dma_start(gw[:, :], gate_w).then_inc(s_ew, 16)
            sp.dma_start(gb[:, :], gate_b).then_inc(s_ew, 16)

            def pair_loads(c, first, last):
                i = c.i
                if not last:
                    c.pair(s_xn, 0)
                    sp.dma_start(xa[:, :], x_tb[bass.ds(i * 128 + 128, 128), :]).then_inc(s_xa, 16)
                if not first:
                    c.pair(s_y, -1)
                    sp.dma_start(xb[:, :], x_tb[bass.ds(i * 128, 128), :]).then_inc(s_xb, 16)

            run_pairs(sp, pair_loads)

            def load_x(tile, n):
                sp.dma_start(xo[:, n, :, :], x_tbd[:, bass.ds(tile * FG, FG), :]).then_inc(s_xo[n], 16)

            def store_and_reload(c, first, last):
                for n in range(2):
                    c.at_least(s_fr, 2, n + 1)
                    sp.dma_start(out[:, bass.ds(c.i * (2 * FG) + n * FG, FG), :], res[:, n, :, :])\
                        .then_inc(s_out[n], 16)
                    c.at_least(s_out[n], 16, 16)
                    if not last:
                        load_x(c.i * 2 + (n + 2), n)

            for n in range(2):
                load_x(n, n)
            run_tiles(sp, store_and_reload)
        @block.gpsimd
        def _(pool):
            pool.memset(kst[:, :, Q * S:], 0.0).then_inc(s_kc, 1)
            pool.memset(mhalf[:, :], -0.5).then_inc(s_pm, 1)
            pool.memset(zsum[:, :], 0.0).then_inc(s_zs, 1)

            def rstd(wait, mv, ve, rs, s_ve, s_rs, wait_ve, hold=lambda: None):
                wait()
                hold()
                pool.tensor_scalar(ve[:, :], mv[:, 1:2], EPS, None, ALU.add).then_inc(s_ve, 1)
                wait_ve()
                pool.tensor_tensor(rs[:, :], ve[:, :], mhalf[:, :], ALU.pow).then_inc(s_rs, 1)

            pool.wait_ge(s_pm, 1)
            rstd(lambda: pool.wait_ge(s_x2, 1), mv1, ve1, rs1, s_xv, s_xs, lambda: pool.wait_ge(s_xv, 1))
            for k in range(KSTEPS):
                pool.wait_ge(s_kvm, k + 1)
                part = kst[:, k * KG:(k + 1) * KG, :]
                pool.tensor_tensor(part[:, :, 2 * S:3 * S], kr[:, k % 2, :, :], part[:, :, S:2 * S],
                                   ALU.subtract).then_inc(s_kl, 1)

            def save_attn(c, k):
                for g in range(G):
                    c.turn(s_at, TURNS * (k + 1) - G + g)
                i = c.i
                dst = ctx_attn[:, :, bass.ds((i + k) * U, U)].rearrange("p b u -> p u b")
                pool.tensor_copy(dst, at[:, :, :]).then_inc(s_sv, 1)

            def finish(c, k, even):
                rstd(lambda: c.pair(s_y2, k), mv2, ve2, rs2, s_yv, s_ys, lambda: c.pair(s_yv, k),
                     c.hold)
                c.pair(s_z, k)
                c.pair(s_zs, k)
                pool.tensor_tensor(zsum[:, :], zsum[:, :], z[:, :], ALU.add).then_inc(s_zs, 1)

            def pair_work(c, first, last):
                if not first:
                    save_attn(c, -1)
                if not last:
                    rstd(lambda: c.pair(s_x2, 1), mv1, ve1, rs1, s_xv, s_xs, lambda: c.pair(s_xv, 1),
                         c.hold)
                if not first:
                    finish(c, -1, True)

            run_pairs(pool, pair_work)
            c = Counts(pool, PAIRS - 1)
            save_attn(c, 0)
            finish(c, 0, True)

        @block.scalar
        def _(act):
            act.dma_start(wf[:, :, :], w_gates).then_inc(s_w, 16)
            act.dma_start(bi[:, :, :], b_ih).then_inc(s_w, 16)
            act.dma_start(bh[:, :, :], b_hh).then_inc(s_w, 16)
            act.dma_start(bo[:, :], b_out).then_inc(s_w, 16)
            act.dma_start(xa[:, :], x_tb[0:128, :]).then_inc(s_xa, 16)
            for k in range(KSTEPS + 1):
                if k < KSTEPS:
                    p, rows = k % 2, slice(k * KG, (k + 1) * KG)
                    act.wait_ge(s_kvp, k + 1)
                    if k >= 2:
                        act.wait_ge(s_vl, k - 1)
                    act.activation(kst[:, rows, 0:S], bank[p][:, 0:KG * S].rearrange("p (b s) -> p b s", b=KG),
                                   ACT.Copy, scale=0.5)
                    act.copy(v0hi[:, p, :, :], bank[2 + p][:, :].rearrange("p (b j) -> p b j", b=KG))
                    act.copy(v1hi[:, p, :, :], bank[4 + p][:, :].rearrange("p (b j) -> p b j", b=KG))\
                        .then_inc(s_kvh, 1)
                if k >= 1:
                    p, rows = (k - 1) % 2, slice((k - 1) * KG, k * KG)
                    act.wait_ge(s_kvr, k)
                    act.copy(kst[:, rows, S:2 * S], kr[:, p, :, :])
                    act.copy(v1mid[:, p, :, :], v1r[:, p, :, :]).then_inc(s_kvm, 1)
            act.wait_ge(s_xT, 1)

            def x_hi(u):
                cols = slice(u * B, (u + 1) * B)
                act.copy(xq[:, 0, cols], ps_xT[:, cols]).then_inc(s_xh, 1)

            x_hi(0)
            act.wait_ge(s_xl, 1)
            x_hi(1)

            def gates(c, k, g):
                c.turn(s_gates, k)
                act.activation(tg[g][:, :, :], ps_gates[g], ACT.Tanh).then_inc(s_tg, 1)
                c.turn(s_c, k)
                act.activation(tc[g][:, :], c2[g][:, :], ACT.Tanh, scale=0.5).then_inc(s_tc, 1)

            def exps(c, k, g):
                c.turn(s_mx, k)
                act.activation(expo[g][:, 0:S], ps_row[g][:, 0:S], ACT.Exp, bias=neg_max[g][:, 0:1],
                               accum_out=den[g][:, 0:1])
                act.activation(expo[g][:, S:SD], ps_row[g][:, S:SD], ACT.Exp, bias=neg_max[g][:, 0:1])\
                    .then_inc(s_ex, 1)

            def attn(c, k, g, u):
                c.turn(s_vs, k)
                act.activation(atq[g][:, 0, :], at_in[g][:, :], ACT.Tanh, bias=bo[:, 0:1])
                c.pair(s_sv, -1)
                c.pair(s_yT, -1)
                act.activation(at[:, u, g * NB:(g + 1) * NB], at_in[g][:, :], ACT.Tanh, bias=bo[:, 0:1])\
                    .then_inc(s_at, 1)

            def store_z(c, k):
                c.pair(s_zT, k)
                i = c.i
                dst = zT[:, :, bass.ds((i + k) * U, U)].rearrange("p b u -> p u b")
                act.copy(dst, ps_zT.rearrange("p (u b) -> p u b", u=U)).then_inc(s_zc, 1)

            def pair_work(c, first, last):
                for u in range(U):
                    for g in range(G):
                        gates(c, u * G + g, g)
                    for g in range(G):
                        exps(c, u * G + g, g)
                    attn(c, u * G, 0, u)
                    if not last:
                        c.step(s_xg, u)
                        c.pair(s_xT, 1)
                        c.step(s_xl, U - 1 + u)
                        x_hi(u)
                    if u == 1 and not first:
                        store_z(c, -1)
                    for g in range(1, G):
                        attn(c, u * G + g, g, u)

            run_pairs(act, pair_work)
            store_z(Counts(act, PAIRS - 1), 0)

            act.wait_ge(s_gv, 3)
            act.activation(ge[:, :], lg[:, :], ACT.Exp, bias=ntop[:, 0:1]).then_inc(s_ga, 1)

            def tiles(c, first, last):
                for n in range(2 * E):
                    c.at_least(s_fp, 2 * E, n + 1)
                    c.at_least(s_fa, 2 * E, n - 4 + 1)
                    act.activation(gl[:, n % 4, :, :], bank[n % 4][:, :].rearrange("p (b t) -> p b t", b=FG),
                                   ACT.Gelu, bias=eb[:, n % E:n % E + 1]).then_inc(s_fg, 1)

            run_tiles(act, tiles)

        @block.vector
        def _(dve):
            dve.memset(ones[:, :], 1.0).then_inc(s_ms, 1)
            dve.memset(onesf[:, :], 1.0)
            for g in range(G):
                dve.memset(c2[g][:, :], 0.0)
                dve.memset(hq[g][:, :, :], 0.0)
                dve.memset(atq[g][:, :, :], 0.0)
                if g < G - 1:
                    dve.memset(alpha[g][:, :, :], 0.0)
            dve.memset(alpha[G - 1][:, :, :], 0.0).then_inc(s_ms, 1)

            dve.wait_ge(s_w, 16 * 7)
            for kind, blocks, factor in ((0, (0, 1, 3), 0.5), (1, (0, 1, 3), 0.5),
                                         (2, (0, 1, 3), 0.25), (2, (2,), 0.5), (3, (0,), 0.5)):
                for m in blocks:
                    w = wf[:, 4 * kind + m, :]
                    dve.tensor_scalar(w, w, factor, None, ALU.mult).then_inc(s_ws, 1)
            dve.tensor_tensor(bi[:, :, :], bi[:, :, :], bh[:, :, :], ALU.add).then_inc(s_b, 1)
            dve.wait_ge(s_b, 1)
            for m in (0, 1, 3):
                dve.tensor_scalar(bi[:, m, :], bi[:, m, :], 0.5, None, ALU.mult).then_inc(s_b, 1)
            dve.wait_ge(s_ws, 11)
            dve.tensor_copy(w3[:, 0, :, :], wf[:, :, :]).then_inc(s_wh, 1)
            dve.wait_ge(s_b, 4)
            dve.tensor_copy(bhi[:, :, :], bi[:, :, :]).then_inc(s_b, 1)
            dve.wait_ge(s_wh, 1)
            dve.tensor_tensor(wf[:, :, :], wf[:, :, :], w3[:, 0, :, :], ALU.subtract).then_inc(s_wr, 1)
            dve.wait_ge(s_b, 5)
            dve.scalar_tensor_tensor(out=bh[:, :, :], in0=bhi[:, :, :], scalar=mask(3), in1=bi[:, :, :],
                                     op0=ALU.mult, op1=ALU.add).then_inc(s_b, 1)
            dve.wait_ge(s_wr, 1)
            dve.tensor_copy(w3[:, 1, :, :], wf[:, :, :]).then_inc(s_wm, 1)
            dve.wait_ge(s_b, 6)
            dve.tensor_copy(bhi[:, :, :], bh[:, :, :]).then_inc(s_b, 1)
            dve.wait_ge(s_wm, 1)
            dve.tensor_tensor(w3[:, 2, :, :], wf[:, :, :], w3[:, 1, :, :], ALU.subtract).then_inc(s_wl, 1)
            dve.wait_ge(s_b, 7)
            dve.scalar_tensor_tensor(out=b3[:, :, :], in0=bhi[:, :, :], scalar=mask(4), in1=bh[:, :, :],
                                     op0=ALU.mult, op1=ALU.add).then_inc(s_wl, 1)

            def ln1_stats(wait_x, wait_stats, hold=lambda: None):
                wait_x()
                dve.bn_stats(st1[:, :], xa[:, :]).then_inc(s_x1, 1)
                wait_stats()
                hold()
                dve.bn_aggr(mv1[:, :], st1[:, :]).then_inc(s_x2, 1)

            def ln1_apply(wait_rstd, wait_xn_read):
                wait_rstd()
                wait_xn_read()
                dve.tensor_scalar(xn[:, :], xa[:, :], mv1[:, 0:1], rs1[:, 0:1], ALU.subtract, ALU.mult)\
                    .then_inc(s_xn, 1)

            def x_parts(c, k, u):
                cols = slice(u * B, (u + 1) * B)
                c.step(s_xh, k)
                dve.tensor_tensor(xr[:, cols], ps_xT[:, cols], xq[:, 0, cols], ALU.subtract)
                dve.tensor_tensor(xq[:, 1, cols], ps_xT[:, cols], xq[:, 0, cols], ALU.subtract).then_inc(s_xm, 1)
                c.step(s_xm, k)
                dve.tensor_tensor(xq[:, 2, cols], xr[:, cols], xq[:, 1, cols], ALU.subtract).then_inc(s_xl, 1)

            ln1_stats(lambda: dve.wait_ge(s_xa, 16), lambda: dve.wait_ge(s_x1, 1))
            ln1_apply(lambda: dve.wait_ge(s_xs, 1), lambda: None)

            for k in range(KSTEPS + 1):
                if k < KSTEPS:
                    p, rows = k % 2, slice(k * KG, (k + 1) * KG)
                    dve.wait_ge(s_kvh, k + 1)
                    if k >= 2:
                        dve.wait_ge(s_kl, k - 1)
                        dve.wait_ge(s_vl, k - 1)
                    dve.scalar_tensor_tensor(
                        out=kr[:, p, :, :], in0=bank[p][:, 0:KG * S].rearrange("p (b s) -> p b s", b=KG),
                        scalar=0.5, in1=kst[:, rows, 0:S], op0=ALU.mult, op1=ALU.subtract)
                    dve.scalar_tensor_tensor(
                        out=v1r[:, p, :, :], in0=v1hi[:, p, :, :], scalar=mask(1),
                        in1=bank[4 + p][:, :].rearrange("p (b j) -> p b j", b=KG),
                        op0=ALU.mult, op1=ALU.add)
                    dve.scalar_tensor_tensor(
                        out=vst[:, rows, 0, :], in0=v0hi[:, p, :, :], scalar=mask(0),
                        in1=bank[2 + p][:, :].rearrange("p (b j) -> p b j", b=KG),
                        op0=ALU.mult, op1=ALU.add).then_inc(s_kvr, 1)
                if k >= 1:
                    p, rows = (k - 1) % 2, slice((k - 1) * KG, k * KG)
                    dve.wait_ge(s_kvm, k)
                    dve.scalar_tensor_tensor(
                        out=vst[:, rows, 1, :], in0=v1mid[:, p, :, :], scalar=mask(2), in1=v1r[:, p, :, :],
                        op0=ALU.mult, op1=ALU.add).then_inc(s_vl, 1)
            for u in range(U):
                x_parts(Counts(dve, 0), u, u)

            def cell(c, k, g):
                t_in, t_forget, t_cell, t_out = (tg[g][:, m, :] for m in range(4))
                c.turn(s_tg, k)
                dve.scalar_tensor_tensor(out=in_term[g][:, :], in0=t_in, scalar=1.0, in1=t_cell,
                                         op0=ALU.add, op1=ALU.mult)
                dve.scalar_tensor_tensor(out=forget_term[g][:, :], in0=t_forget, scalar=1.0, in1=c2[g][:, :],
                                         op0=ALU.add, op1=ALU.mult).then_inc(s_ct, 1)
                c.turn(s_ct, k)
                dve.scalar_tensor_tensor(out=c2[g][:, :], in0=forget_term[g][:, :], scalar=0.5,
                                         in1=in_term[g][:, :], op0=ALU.mult, op1=ALU.add).then_inc(s_c, 1)
                c.turn(s_tc, k)
                dve.scalar_tensor_tensor(out=hq[g][:, 0, :], in0=t_out, scalar=1.0, in1=tc[g][:, :],
                                         op0=ALU.add, op1=ALU.mult)
                dve.scalar_tensor_tensor(out=h2[g][:, :], in0=t_out, scalar=1.0, in1=tc[g][:, :],
                                         op0=ALU.add, op1=ALU.mult).then_inc(s_h, 1)
                c.turn(s_h, k)
                dve.tensor_tensor(hr[g][:, :], h2[g][:, :], hq[g][:, 0, :], ALU.subtract)
                dve.tensor_tensor(hq[g][:, 1, :], h2[g][:, :], hq[g][:, 0, :], ALU.subtract).then_inc(s_hm, 1)
                c.turn(s_hm, k)
                dve.tensor_tensor(hq[g][:, 2, :], hr[g][:, :], hq[g][:, 1, :], ALU.subtract).then_inc(s_hl, 1)

            def score_sum(c, k, g):
                c.turn(s_sp, k)
                dve.tensor_reduce(sc[g][:, :, :], ps_sc[g], AX_X, ALU.add).then_inc(s_ss, 1)

            def softmax(c, k, g):
                c.turn(s_row, k)
                dve.tensor_reduce(neg_max[g][:, :], ps_row[g][:, 0:S], AX_X, ALU.max, negate=True)\
                    .then_inc(s_mx, 1)
                c.turn(s_ex, k)
                dve.reciprocal(rden[g][:, :], den[g][:, :]).then_inc(s_rd, 1)
                c.turn(s_rd, k)
                dve.tensor_scalar(alpha[g][:, 0, :].rearrange("p (k s) -> p k s", k=2),
                                  expo[g][:, 0:SA].unsqueeze(1).to_broadcast([NB, 2, SA]),
                                  rden[g][:, 0:1], None, ALU.mult)
                dve.tensor_scalar(alpha[g][:, 1, 0:SD], expo[g][:, :], rden[g][:, 0:1], None, ALU.mult)\
                    .then_inc(s_al, 1)

            def alpha_parts(c, k, g):
                c.turn(s_aT, k)
                dve.tensor_copy(aq[g][:, 0, :, :], ps_alT[g]).then_inc(s_ah, 1)
                c.turn(s_ah, k)
                dve.tensor_tensor(ar[g][:, :, :], ps_alT[g], aq[g][:, 0, :, :], ALU.subtract)
                dve.tensor_tensor(aq[g][:, 1, :, :], ps_alT[g], aq[g][:, 0, :, :], ALU.subtract)\
                    .then_inc(s_am, 1)
                c.turn(s_am, k)
                dve.tensor_tensor(aq[g][:, 2, :, :], ar[g][:, :, :], aq[g][:, 1, :, :], ALU.subtract)\
                    .then_inc(s_as, 1)

            def value_sum(c, k, g):
                c.turn(s_vp, k)
                dve.tensor_reduce(at_in[g][:, :], ps_val[g], AX_X, ALU.add).then_inc(s_vs, 1)

            def attn_parts(c, k, g, u):
                c.turn(s_at, k)
                cols = at[:, u, g * NB:(g + 1) * NB]
                dve.tensor_tensor(at_r[g][:, :], cols, atq[g][:, 0, :], ALU.subtract)
                dve.tensor_tensor(atq[g][:, 1, :], cols, atq[g][:, 0, :], ALU.subtract).then_inc(s_tm, 1)
                c.turn(s_tm, k)
                dve.tensor_tensor(atq[g][:, 2, :], at_r[g][:, :], atq[g][:, 1, :], ALU.subtract)\
                    .then_inc(s_ts, 1)

            def ln2_stats(c, k):
                c.pair(s_yT, k)
                c.pair(s_xb, k, 16)
                dve.tensor_tensor(y[:, :], ps_y, xb[:, :], ALU.add).then_inc(s_y, 1)
                c.pair(s_y, k)
                dve.bn_stats(st2[:, :], y[:, :]).then_inc(s_y1, 1)
                c.pair(s_y1, k)
                c.hold()
                dve.bn_aggr(mv2[:, :], st2[:, :]).then_inc(s_y2, 1)

            def ln2_apply(c, k):
                c.pair(s_ys, k)
                dve.tensor_scalar(z[:, :], y[:, :], mv2[:, 0:1], rs2[:, 0:1], ALU.subtract, ALU.mult)\
                    .then_inc(s_z, 1)

            def pair_work(c, first, last):
                for u in range(U):
                    for g in range(G):
                        cell(c, u * G + g, g)
                    if u == 0 and not last:
                        ln1_stats(lambda: c.pair(s_xa, 1, 16), lambda: c.pair(s_x1, 1), c.hold)
                    if u == 1 and not first:
                        ln2_stats(c, -1)
                    score_sum(c, u * G, 0)
                    softmax(c, u * G, 0)
                    if u == 0 and not last:
                        ln1_apply(lambda: c.pair(s_xs, 1), lambda: c.pair(s_xT, 0))
                    if u == 1 and not first:
                        ln2_apply(c, -1)
                    for g in range(1, G):
                        score_sum(c, u * G + g, g)
                    alpha_parts(c, u * G, 0)
                    for g in range(1, G):
                        softmax(c, u * G + g, g)
                    value_sum(c, u * G, 0)
                    for g in range(1, G):
                        alpha_parts(c, u * G + g, g)
                    attn_parts(c, u * G, 0, u)
                    if not last:
                        x_parts(c, U + u, u)
                    for g in range(1, G):
                        value_sum(c, u * G + g, g)
                        attn_parts(c, u * G + g, g, u)

            run_pairs(dve, pair_work)
            c = Counts(dve, PAIRS - 1)
            ln2_stats(c, 0)
            ln2_apply(c, 0)

            dve.wait_ge(s_gt, 1)
            dve.tensor_copy(pooled[:, :], bank[4][:, 0:B]).then_inc(s_gv, 1)
            dve.wait_ge(s_gt, 2)
            dve.wait_ge(s_ew, 64)
            dve.tensor_tensor(lg[:, :], bank[4][0:B, B:B + E], gb[:, :], ALU.add).then_inc(s_gv, 1)
            dve.wait_ge(s_gv, 2)
            dve.max(top[:, :], lg[:, :]).then_inc(s_b, 1)
            dve.wait_ge(s_b, 8)
            dve.tensor_scalar(ntop[:, :], top[:, 0:1], -1.0, None, ALU.mult).then_inc(s_gv, 1)
            dve.tensor_scalar(keep[:, :], lg[:, :], top[:, 1:2], None, ALU.is_ge).then_inc(s_b, 1)
            dve.wait_ge(s_ga, 1)
            dve.wait_ge(s_b, 9)
            dve.tensor_tensor(gk[:, :], ge[:, :], keep[:, :], ALU.mult).then_inc(s_b, 1)
            dve.wait_ge(s_b, 10)
            dve.tensor_reduce(gs[:, :], gk[:, :], AX_X, ALU.add).then_inc(s_b, 1)
            dve.wait_ge(s_b, 11)
            dve.reciprocal(gr[:, :], gs[:, :]).then_inc(s_b, 1)
            dve.wait_ge(s_b, 12)
            dve.tensor_scalar(ge[:, :], gk[:, :], gr[:, 0:1], None, ALU.mult).then_inc(s_b, 1)
            dve.wait_ge(s_b, 13)
            dve.tensor_tensor(gd[:, :, :], ge[:, :].unsqueeze(1).to_broadcast([B, B, E]),
                              cst[0:B, C_ID:C_ID + B].unsqueeze(2).to_broadcast([B, B, E]), ALU.mult)\
                .then_inc(s_gv, 1)
            dve.wait_ge(s_gt, 3)
            dve.tensor_copy(gates[:, :, :], bank[5][:, :].rearrange("p (b e) -> p b e", e=E)).then_inc(s_gv, 1)
            dve.wait_ge(s_gv, 5)

            def add_expert(c, n, e):
                c.at_least(s_fg, 2 * E, n * E + e + 1)
                c.at_least(s_fa, 2 * E, n * E + e)
                if e == 0:
                    c.at_least(s_fT, 2, n - 1)
                for q in range(FG):
                    row = c.i * (2 * FG) + (n * FG + q)
                    before = ctx_attn[:, bass.ds(row, 1), :] if e == 0 else acc[:, n, q:q + 1, :]
                    last = dve.scalar_tensor_tensor(
                        out=acc[:, n, q:q + 1, :], in0=gl[:, (n * E + e) % 4, q:q + 1, :],
                        scalar=gates[:, bass.ds(row, 1), e], in1=before, op0=ALU.mult, op1=ALU.add)
                last.then_inc(s_fa, 1)

            def result(c, n, ago):
                p, back = (n - ago) % 2, (1 if ago > n else 0)
                c.at_least(s_fT, 2, n - ago + 1)
                c.at_least(s_xo[p], 16, 16 * (1 - back))
                dve.tensor_tensor(res[:, p, :, :], bank[6 + p][:, :].rearrange("p (b d) -> p b d", b=FG),
                                  xo[:, p, :, :], ALU.add).then_inc(s_fr, 1)

            def tiles(c, first, last):
                for n in range(2):
                    for e in range(E):
                        add_expert(c, n, e)
                        if e == 5 and not (first and n == 0):
                            result(c, n, 1)
                if last:
                    result(c, 1, 0)

            run_tiles(dve, tiles)

        @block.tensor
        def _(pe):
            mm = pe.matmul
            pe.wait_ge(s_w, 16 * 7)
            for k in range(KSTEPS):
                p = k % 2
                if k % (KSTEPS // 4) == 0:
                    pe.wait_ge(s_ctx[k // (KSTEPS // 4)], 16)
                if k >= 2:
                    pe.wait_ge(s_kvr, k - 1)
                mm(bank[p][:, 0:KG * S], wq[:, :], ctx_attn[:, k * KG:(k + 1) * KG, 0:S], start=True, stop=True)
                for q in range(KG):
                    b = k * KG + q
                    cols = slice(q * 128, (q + 1) * 128)
                    for half in range(2):
                        mm(bank[2 + p][half * SA:(half + 1) * SA, cols], ctx_attn[:, b, 0:SA], wo[:, :],
                           start=True, stop=True)
                    last = mm(bank[4 + p][:, cols], ctx_attn[:, b, :], wo[:, :], start=True, stop=True)
                last.then_inc(s_kvp, 1)
            pe.wait_ge(s_kvr, KSTEPS)
            pe.wait_ge(s_xn, 1)
            pe.transpose(ps_xT, xn[:, :], ident).then_inc(s_xT, 1)

            def early_gates(g, u):
                o = ps_gates[g]
                for m in range(4):
                    mm(o[:, m, :], b3[:, m, :], ones[:, 0:NB], start=(m == 0), stop=False, skip_group_check=True)
                    for wp, xp in PRODUCTS:
                        cols = slice(u * B + g * NB, u * B + (g + 1) * NB)
                        last = mm(o[:, m, :], w3[:, wp, m, :], xq[:, xp, cols],
                                  start=False, stop=False, skip_group_check=True)
                if g == G - 1:
                    last.then_inc(s_xg, 1)
                for m in range(4):
                    for wp, hp in PRODUCTS:
                        mm(o[:, m, :], w3[:, wp, 8 + m, :], hq[g][:, hp, :], start=False, stop=False,
                           skip_group_check=True)

            def attn_gates(c, k, g):
                c.turn(s_ts, k - G)
                o = ps_gates[g]
                for m in range(4):
                    for wp, ap in PRODUCTS:
                        last = mm(o[:, m, :], w3[:, wp, 4 + m, :], atq[g][:, ap, :], start=False,
                                  stop=(wp, ap) == PRODUCTS[-1], skip_group_check=True)
                last.then_inc(s_gates, 1)

            def scores(c, k, g):
                c.turn(s_hl, k)
                for j in range(NB):
                    for pack in range(2):
                        last = mm(ps_sc[g][:, pack, j, :], kst[:, g * NB + j, pack * 128:(pack + 1) * 128],
                                  hq[g][:, :, j], start=True, stop=True)
                last.then_inc(s_sp, 1)

            def h_out(g, opens):
                for n, (wp, hp) in enumerate(PRODUCTS):
                    mm(ps_val[g][:, :, 0], w3[:, wp, 12, :], hq[g][:, hp, :], start=(opens and n == 0),
                       stop=False, skip_group_check=True)

            def rows(c, k, g):
                c.turn(s_ss, k)
                for pack in range(2):
                    last = mm(ps_row[g], sc[g][:, pack, :], sel(pack), start=(pack == 0), stop=(pack == 1))
                last.then_inc(s_row, 1)

            def turn_alpha(c, k, g):
                c.turn(s_al, k)
                c.hold()
                id_nb = cst[0:NB, C_ID:C_ID + NB]
                for pack in range(2):
                    last = pe.transpose(ps_alT[g][:, pack, :], alpha[g][:, pack, :], id_nb)
                last.then_inc(s_aT, 1)

            def values(c, k, g):
                c.turn(s_as, k)
                for j in range(NB):
                    for pack in range(2):
                        last = mm(ps_val[g][:, j, :], vst[:, g * NB + j, pack, :], aq[g][:, :, pack, j],
                                  start=False, stop=(pack == 1), skip_group_check=True)
                last.then_inc(s_vp, 1)

            pe.wait_ge(s_wl, 2)
            pe.wait_ge(s_xl, U)
            pe.wait_ge(s_ms, 2)
            pe.wait_ge(s_kc, 1)
            pe.wait_ge(s_kl, KSTEPS)
            pe.wait_ge(s_vl, KSTEPS)
            early_gates(0, 0)

            def pair_work(c, first, last):
                for u in range(U):
                    last_step = last and u == U - 1
                    k0, k1 = u * G, u * G + 1
                    attn_gates(c, k0, 0)
                    c.turn(s_vs, k1 - G)
                    early_gates(1, u)
                    attn_gates(c, k1, 1)
                    if u == 0 and not first:
                        pe.transpose(ps_y, at[:, :, :].rearrange("p u b -> p (u b)"), ident).then_inc(s_yT, 1)
                    scores(c, k0, 0)
                    if not last_step:
                        c.step(s_xl, u + 1)
                        early_gates(0, 1 - u)
                    h_out(0, last_step)
                    rows(c, k0, 0)
                    scores(c, k1, 1)
                    turn_alpha(c, k0, 0)
                    rows(c, k1, 1)
                    h_out(1, False)
                    if u == 0 and not last:
                        c.pair(s_xn, 1)
                        c.step(s_xl, U - 1)
                        pe.transpose(ps_xT, xn[:, :], ident).then_inc(s_xT, 1)
                    if u == 1 and not first:
                        c.pair(s_z, -1)
                        pe.transpose(ps_zT, z[:, :], ident).then_inc(s_zT, 1)
                    values(c, k0, 0)
                    turn_alpha(c, k1, 1)
                    values(c, k1, 1)

            run_pairs(pe, pair_work)
            c = Counts(pe, PAIRS - 1)
            for g in range(G):
                c.turn(s_at, TURNS - G + g)
            c.pair(s_y, -1)
            pe.transpose(ps_y, at[:, :, :].rearrange("p u b -> p (u b)"), ident).then_inc(s_yT, 1)
            c.pair(s_z, 0)
            c.pair(s_zc, -1)
            pe.transpose(ps_zT, z[:, :], ident).then_inc(s_zT, 1)

            pe.wait_ge(s_zs, PAIRS + 1)
            pe.wait_ge(s_ew, 64)
            mm(bank[4][:, 0:B], zsum[:, :], fold, start=True, stop=True).then_inc(s_gt, 1)
            pe.wait_ge(s_gv, 1)
            mm(bank[4][0:B, B:B + E], pooled[:, :], gw[:, :], start=True, stop=True).then_inc(s_gt, 1)
            pe.wait_ge(s_gv, 4)
            mm(bank[5][:, :], onesf[:, :], gd[:, :, :].rearrange("p b e -> p (b e)"), start=True, stop=True)\
                .then_inc(s_gt, 1)
            pe.wait_ge(s_zc, PAIRS)

            def tile_back(c, n, ago):
                p = (n - ago) % 2
                c.at_least(s_fa, 2 * E, (n - ago + 1) * E)
                for q in range(FG):
                    last = pe.transpose(bank[6 + p][:, q * 128:(q + 1) * 128], acc[:, p, q, :], ident)
                last.then_inc(s_fT, 1)

            def tiles(c, first, last):
                for n in range(2):
                    for e in range(E):
                        k = n * E + e
                        c.at_least(s_fg, 2 * E, k - 4 + 1)
                        pe.matmul(bank[k % 4][:, :], ew[:, e, :],
                                  zT[:, bass.ds(c.i * (2 * FG) + n * FG, FG), :].rearrange("p b t -> p (b t)"),
                                  start=True, stop=True).then_inc(s_fp, 1)
                        if e == 4 and not (first and n == 0):
                            tile_back(c, n, 1)
                if last:
                    tile_back(c, 1, 0)

            run_tiles(pe, tiles)


def kernel(x, ctx_1024, L0_xattn_W_ih, L0_xattn_W_hh, L0_xattn_b_ih, L0_xattn_b_hh, L0_xattn_Wq,
           L0_xattn_Wout, L0_xattn_b_out, L0_ffn_gate_w, L0_ffn_gate_b, L0_ffn_expert_w, L0_ffn_expert_b):
    import concourse.bacc as bacc
    from concourse.bass_utils import run_bass_kernel_spmd as run

    x, context = np.asarray(x), np.asarray(ctx_1024)
    w_ih, w_hh, w_out = (np.asarray(a) for a in (L0_xattn_W_ih, L0_xattn_W_hh, L0_xattn_Wout))
    c_t = context.transpose(2, 0, 1)
    ctx_dup = np.zeros((D, B, 128), np.float32)
    ctx_dup[:, :, :S] = c_t
    for k in (1, 2):
        ctx_dup[:, :, SA + k * SB:SA + (k + 1) * SB] = c_t[:, :, SA:]
    w_gates = np.concatenate([w_ih[:, :D].T, w_ih[:, D:].T, w_hh.T, w_out[:, D:].T], axis=1)

    def bias_rows(b):
        rows = np.zeros((128, 4 * 128), np.float32)
        rows[[0, 32, 64]] = np.asarray(b)
        return rows.reshape(128, 4, 128)

    arrays = {
        "x_tbd": x.transpose(1, 0, 2),
        "ctx_dup": ctx_dup,
        "w_gates": w_gates.reshape(128, 13, 128),
        "b_ih": bias_rows(L0_xattn_b_ih),
        "b_hh": bias_rows(L0_xattn_b_hh),
        "w_q": np.asarray(L0_xattn_Wq),
        "w_out": w_out[:, :D].T,
        "b_out": np.asarray(L0_xattn_b_out).reshape(128, 1),
        "gate_w": np.asarray(L0_ffn_gate_w).T,
        "gate_b": np.repeat(np.asarray(L0_ffn_gate_b)[None, :], B, axis=0),
        "expert_w": np.asarray(L0_ffn_expert_w).transpose(2, 0, 1),
        "expert_b": np.asarray(L0_ffn_expert_b).T,
        "consts": constants(),
    }
    arrays = {k: np.ascontiguousarray(v) for k, v in arrays.items()}
    nc = bacc.Bacc("TRN2", target_bir_lowering=False, num_devices=1)
    ins = {k: nc.dram_tensor(f"in_{k}", v.shape, mybir.dt.from_np(v.dtype), kind="ExternalInput").ap()
           for k, v in arrays.items()}
    out = nc.dram_tensor("out", (T, B, D), F32, kind="ExternalOutput").ap()
    xattn_moe(nc, **ins, out=out)
    got = run(nc, [{f"in_{k}": v for k, v in arrays.items()}], core_ids=[0]).results[0]["out"]
    return np.ascontiguousarray(np.asarray(got).transpose(1, 0, 2))
```

```python
from contextlib import ExitStack

import numpy as np

import concourse.bass as bass
from concourse import mybir

ALU = mybir.AluOpType
ACT = mybir.ActivationFunctionType
AX_X = mybir.AxisListType.X
F32 = mybir.dt.float32
BF16 = mybir.dt.bfloat16

B, T, D, S, E = 64, 128, 128, 77, 8
H = D
EPS = 1e-5
G = 2
NB = B // G
U = 2
PAIRS = T // U
TURNS = U * G
Q = 3
SA = 64
SB = S - SA
SD = SA + Q * SB
PRODUCTS = ((2, 0), (1, 1), (0, 2), (1, 0), (0, 1), (0, 0))
WITH_HI = tuple(p for p in PRODUCTS if p[1] == 0)
WITHOUT_HI = tuple(p for p in PRODUCTS if p[1] > 0)
KG = 4
KSTEPS = B // KG
FG = 4
FTILES = B // FG
FV = FG - 1

C_ID = 0
C_SEL = C_ID + 128
C_FOLD = C_SEL + 2 * S
C_MASK = C_FOLD + B
C_ALL = C_MASK + 5


def constants():
    c = np.zeros((128, C_ALL), np.float32)
    c[:, C_ID:C_ID + 128] = np.eye(128)
    for col in range(Q * S):
        c[col % 128, C_SEL + (col // 128) * S + col % S] = 1
    for r in range(128):
        c[r, C_FOLD + r % B] = 1.0 / T
    c[SA:, C_MASK + 0] = -1
    c[:SA, C_MASK + 1] = -1
    c[SA + SB:, C_MASK + 1] = -1
    c[:SA, C_MASK + 2] = -1
    c[SA + 2 * SB:, C_MASK + 2] = -1
    c[32:, C_MASK + 3] = -1
    c[64:, C_MASK + 4] = -1
    return c


def xattn_moe(nc, x_tbd, ctx_dup, w_gates, b_ih, b_hh, w_q, w_out, b_out,
              gate_w, gate_b, expert_w, expert_b, consts, out):
    x_tb = x_tbd.rearrange("t b d -> (t b) d")
    with ExitStack() as ctx:
        def sb(name, shape, dt):
            return ctx.enter_context(nc.sbuf_tensor(name, shape, dt))

        def sem(name):
            return ctx.enter_context(nc.semaphore(name))

        cst = sb("cst", [128, C_ALL], F32)
        ident = cst[:, C_ID:C_ID + 128]
        fold = cst[:, C_FOLD:C_FOLD + B]

        def sel(pack):
            return cst[:, C_SEL + pack * S:C_SEL + (pack + 1) * S]

        def mask(n):
            return cst[:, C_MASK + n:C_MASK + n + 1]

        ctx_attn = sb("ctx_attn", [128, B * 128], F32)
        ctxT = ctx_attn[:, :].rearrange("p (b s) -> p b s", b=B)
        attn_all = ctx_attn[:, :].rearrange("p (t b) -> p t b", t=T)
        kst = sb("kst", [128, B, 2 * 128], BF16)
        vst = sb("vst", [128, B, 2, 128], BF16)
        zT = sb("zT", [128, B, T], F32)
        wf = sb("wf", [128, 13, 128], F32)
        w3 = sb("w3", [128, Q, 13, 128], BF16)
        wq = sb("wq", [128, H], F32)
        wo = sb("wo", [128, 128], F32)
        bi = sb("bi", [128, 4, 128], F32)
        bh = sb("bh", [128, 4, 128], F32)
        bhi = sb("bhi", [128, 4, 128], BF16)
        b3 = sb("b3", [128, 4, 128], BF16)
        ones = sb("ones", [128, B], BF16)
        onesf = sb("onesf", [B, 128], F32)
        bo = sb("bo", [128, 1], F32)
        ew = sb("ew", [128, E, 128], F32)
        eb = sb("eb", [128, E], F32)
        gw = sb("gw", [128, E], F32)
        gb = sb("gb", [B, E], F32)
        kr = sb("kr", [128, 2, KG, S], F32)
        v0hi = sb("v0hi", [128, 2, KG, 128], BF16)
        v1hi = sb("v1hi", [128, 2, KG, 128], BF16)
        v1r = sb("v1r", [128, 2, KG, 128], F32)
        v1mid = sb("v1mid", [128, 2, KG, 128], BF16)
        tg = [sb(f"tg{g}", [128, 4, NB], F32) for g in range(G)]
        c2 = [sb(f"c2_{g}", [128, NB], F32) for g in range(G)]
        in_term = [sb(f"in_term{g}", [128, NB], F32) for g in range(G)]
        forget_term = [sb(f"forget_term{g}", [128, NB], F32) for g in range(G)]
        tc = [sb(f"tc{g}", [128, NB], F32) for g in range(G)]
        h2 = [sb(f"h2_{g}", [128, NB], F32) for g in range(G)]
        hr = [sb(f"hr{g}", [128, NB], F32) for g in range(G)]
        hq = [sb(f"hq{g}", [128, Q, NB], BF16) for g in range(G)]
        sc = [sb(f"sc{g}", [128, 2, NB], F32) for g in range(G)]
        neg_max = [sb(f"neg_max{g}", [NB, 1], F32) for g in range(G)]
        expo = [sb(f"expo{g}", [NB, S], F32) for g in range(G)]
        rden = [sb(f"rden{g}", [NB, 1], F32) for g in range(G)]
        alpha = [sb(f"alpha{g}", [NB, 2 * 128], F32) for g in range(G)]
        ar = [sb(f"ar{g}", [128, 2, NB], F32) for g in range(G)]
        aq = [sb(f"aq{g}", [128, Q, 2, NB], BF16) for g in range(G)]
        at_in = [sb(f"at_in{g}", [128, NB], F32) for g in range(G)]
        at_r = [sb(f"at_r{g}", [128, NB], F32) for g in range(G)]
        atq = [sb(f"atq{g}", [128, Q, NB], BF16) for g in range(G)]
        at = sb("at", [128, U * B], F32)
        xa = sb("xa", [128, D], F32)
        xb = sb("xb", [128, D], F32)
        st1 = sb("st1", [128, 6], F32)
        st2 = sb("st2", [128, 6], F32)
        mv1 = sb("mv1", [128, 2], F32)
        mv2 = sb("mv2", [128, 2], F32)
        ve1 = sb("ve1", [128, 1], F32)
        ve2 = sb("ve2", [128, 1], F32)
        rs1 = sb("rs1", [128, 1], F32)
        rs2 = sb("rs2", [128, 1], F32)
        mhalf = sb("mhalf", [128, 1], F32)
        xn = sb("xn", [128, D], F32)
        xq = sb("xq", [128, Q, U * B], BF16)
        xr = sb("xr", [128, U * B], F32)
        y = sb("y", [128, D], F32)
        z = sb("z", [128, D], F32)
        zsum = sb("zsum", [128, D], F32)
        pooled = sb("pooled", [128, B], F32)
        lg = sb("lg", [B, E], F32)
        top = sb("top", [B, 8], F32)
        ntop = sb("ntop", [B, 1], F32)
        keep = sb("keep", [B, E], F32)
        ge = sb("ge", [B, E], F32)
        gk = sb("gk", [B, E], F32)
        gs = sb("gs", [B, 1], F32)
        gr = sb("gr", [B, 1], F32)
        gd = sb("gd", [B, B, E], F32)
        gates = sb("gates", [128, B, E], F32)
        gl = sb("gl", [128, 4, T], F32)
        gated = sb("gated", [128, 2, T], F32)
        acc = sb("acc", [128, 2, FG, T], F32)
        xo = v1r
        res = sb("res", [128, 2, FG, D], F32)

        bank = [ctx.enter_context(nc.psum_tensor(f"bank{n}", [128, 512], F32)) for n in range(8)]
        ps_gates = [bank[g][:, 0:4 * NB].rearrange("p (m b) -> p m b", m=4) for g in range(G)]
        ps_val = [bank[g][:, 4 * NB:(4 + Q) * NB].rearrange("p (b q) -> p b q", q=Q) for g in range(G)]
        ps_sc = [bank[2 + g][:, 0:2 * NB * Q].rearrange("p (k b q) -> p k b q", k=2, q=Q) for g in range(G)]
        ps_row = [bank[2 + g][0:NB, 256:256 + S] for g in range(G)]
        ps_den = [bank[2 + g][0:NB, 448:449] for g in range(G)]
        ps_alT = [bank[2 + g][:, 384:384 + 2 * NB].rearrange("p (k b) -> p k b", k=2) for g in range(G)]
        ps_xT = bank[4][:, 0:128]
        ps_y = bank[5][:, 0:128]
        ps_zT = bank[6][:, 0:128]

        s_w = sem("weights_loaded")
        s_ctx = [sem(f"context_loaded{n}") for n in range(4)]
        s_ew = sem("expert_weights_loaded")
        s_ms = sem("memsets_done")
        s_pm = sem("pool_memsets_done")
        s_kc = sem("kst_cleared")
        s_ws = sem("weights_scaled")
        s_wh = sem("weights_hi")
        s_wr = sem("weights_rest")
        s_wm = sem("weights_mid")
        s_wl = sem("weights_split")
        s_b = sem("bias_chain")
        s_kvp = sem("kv_products")
        s_kvh = sem("kv_hi")
        s_kvr = sem("kv_rest")
        s_kvm = sem("kv_mid")
        s_kl = sem("k_lo")
        s_vl = sem("v_lo")
        s_gates = sem("gates_ready")
        s_tg = sem("gates_tanh")
        s_ct = sem("c_terms")
        s_c = sem("c_ready")
        s_tc = sem("c_tanh")
        s_h = sem("h_hi")
        s_hm = sem("h_mid")
        s_hl = sem("h_split")
        s_sp = sem("score_parts")
        s_ss = sem("score_sums")
        s_row = sem("score_rows")
        s_mx = sem("neg_max_ready")
        s_ex = sem("exp_ready")
        s_rd = sem("rden_ready")
        s_al = sem("alpha_ready")
        s_aT = sem("alpha_transposed")
        s_ah = sem("alpha_hi")
        s_am = sem("alpha_mid")
        s_as = sem("alpha_split")
        s_vp = sem("value_parts")
        s_vs = sem("value_sums")
        s_at = sem("attn_ready")
        s_tm = sem("attn_mid")
        s_ts = sem("attn_split")
        s_xa = sem("xa_loaded")
        s_x1 = sem("ln1_stats")
        s_x2 = sem("ln1_mean_var")
        s_xv = sem("ln1_var_eps")
        s_xs = sem("ln1_rstd")
        s_xn = sem("ln1_ready")
        s_xT = sem("ln1_transposed")
        s_xh = sem("x_hi")
        s_xm = sem("x_mid")
        s_xl = sem("x_split")
        s_xg = sem("x_gates_done")
        s_xb = sem("xb_loaded")
        s_yT = sem("attn_pair_transposed")
        s_y = sem("y_ready")
        s_y1 = sem("ln2_stats")
        s_y2 = sem("ln2_mean_var")
        s_yv = sem("ln2_var_eps")
        s_ys = sem("ln2_rstd")
        s_z = sem("z_ready")
        s_zs = sem("z_summed")
        s_zT = sem("z_transposed")
        s_zc = sem("z_stored")
        s_gt = sem("gating_tensor")
        s_gv = sem("gating_vector")
        s_ga = sem("gating_scalar")
        s_fp = sem("expert_products")
        s_fg = sem("expert_gelu_vector")
        s_fh = sem("expert_gelu_pool")
        s_fv = sem("expert_added_vector")
        s_fm = sem("expert_gated_pool")
        s_fx = sem("expert_added_pool")
        s_fT = sem("tile_transposed")
        s_fr = sem("tile_result")
        s_xo = [sem(f"residual_loaded{n}") for n in range(2)]
        s_held = sem("held")
        s_out = [sem(f"tile_stored{n}") for n in range(2)]

        block = ctx.enter_context(nc.Block())

        class Counts:

            def __init__(self, eng, i):
                self.eng, self.i, self.known = eng, i, {}

            def at_least(self, s, per_pair, n):
                if isinstance(self.i, int):
                    if per_pair * self.i + n > 0:
                        self.eng.wait_ge(s, per_pair * self.i + n)
                    return
                if (per_pair, n) not in self.known:
                    self.known[per_pair, n] = self.eng.snap(self.i * per_pair + n)
                self.eng.wait_ge(s, self.known[per_pair, n])

            def hold(self):
                if not isinstance(self.i, int):
                    self.eng.sem_inc(s_held, 1)

            def turn(self, s, k):
                self.at_least(s, TURNS, k + 1)

            def step(self, s, k):
                self.at_least(s, U, k + 1)

            def pair(self, s, k, by=1):
                self.at_least(s, by, by * (k + 1))

        def run_pairs(eng, body):
            body(Counts(eng, 0), True, False)
            with eng.Fori(1, PAIRS - 1) as i:
                body(Counts(eng, i), False, False)
            body(Counts(eng, PAIRS - 1), False, True)

        def attn_out(u, g):
            return at[:, u * B + g * NB:u * B + (g + 1) * NB]

        def run_tiles(eng, body):
            body(Counts(eng, 0), True, False)
            with eng.Fori(1, FTILES // 2 - 1) as i:
                body(Counts(eng, i), False, False)
            body(Counts(eng, FTILES // 2 - 1), False, True)

        @block.sync
        def _(sp):
            sp.dma_start(cst[:, :], consts).then_inc(s_w, 16)
            sp.dma_start(wo[:, :], w_out).then_inc(s_w, 16)
            sp.dma_start(wq[:, :], w_q).then_inc(s_w, 16)
            for n in range(4):
                part = slice(n * B // 4, (n + 1) * B // 4)
                sp.dma_start(ctxT[:, part, :], ctx_dup[:, part, :]).then_inc(s_ctx[n], 16)
            sp.dma_start(xb[:, :], x_tb[0:128, :]).then_inc(s_xb, 16)
            sp.dma_start(ew[:, :, :], expert_w).then_inc(s_ew, 16)
            sp.dma_start(eb[:, :], expert_b).then_inc(s_ew, 16)
            sp.dma_start(gw[:, :], gate_w).then_inc(s_ew, 16)
            sp.dma_start(gb[:, :], gate_b).then_inc(s_ew, 16)

            def pair_loads(c, first, last):
                i = c.i
                if not last:
                    c.pair(s_xn, 0)
                    sp.dma_start(xa[:, :], x_tb[bass.ds(i * 128 + 128, 128), :]).then_inc(s_xa, 16)
                if not first:
                    c.pair(s_y, -1)
                    sp.dma_start(xb[:, :], x_tb[bass.ds(i * 128, 128), :]).then_inc(s_xb, 16)

            run_pairs(sp, pair_loads)

            def load_x(tile, n):
                sp.dma_start(xo[:, n, :, :], x_tbd[:, bass.ds(tile * FG, FG), :]).then_inc(s_xo[n], 16)

            def store_and_reload(c, first, last):
                for n in range(2):
                    c.at_least(s_fr, 2, n + 1)
                    sp.dma_start(out[:, bass.ds(c.i * (2 * FG) + n * FG, FG), :], res[:, n, :, :])\
                        .then_inc(s_out[n], 16)
                    c.at_least(s_out[n], 16, 16)
                    if not last:
                        load_x(c.i * 2 + (n + 2), n)

            for n in range(2):
                load_x(n, n)
            run_tiles(sp, store_and_reload)
        @block.gpsimd
        def _(pool):
            pool.memset(kst[:, :, Q * S:], 0.0).then_inc(s_kc, 1)
            pool.memset(mhalf[:, :], -0.5).then_inc(s_pm, 1)
            pool.memset(zsum[:, :], 0.0).then_inc(s_zs, 1)

            def rstd(wait, mv, ve, rs, s_ve, s_rs, wait_ve, hold=lambda: None):
                wait()
                hold()
                pool.tensor_scalar(ve[:, :], mv[:, 1:2], EPS, None, ALU.add).then_inc(s_ve, 1)
                wait_ve()
                pool.tensor_tensor(rs[:, :], ve[:, :], mhalf[:, :], ALU.pow).then_inc(s_rs, 1)

            pool.wait_ge(s_pm, 1)
            rstd(lambda: pool.wait_ge(s_x2, 1), mv1, ve1, rs1, s_xv, s_xs, lambda: pool.wait_ge(s_xv, 1))
            for k in range(KSTEPS):
                pool.wait_ge(s_kvm, k + 1)
                part = kst[:, k * KG:(k + 1) * KG, :]
                pool.tensor_tensor(part[:, :, 2 * S:3 * S], kr[:, k % 2, :, :], part[:, :, S:2 * S],
                                   ALU.subtract).then_inc(s_kl, 1)

            def finish(c, k):
                rstd(lambda: c.pair(s_y2, k), mv2, ve2, rs2, s_yv, s_ys, lambda: c.pair(s_yv, k),
                     c.hold)
                c.pair(s_z, k)
                c.pair(s_zs, k)
                pool.tensor_tensor(zsum[:, :], zsum[:, :], z[:, :], ALU.add).then_inc(s_zs, 1)

            def pair_work(c, first, last):
                if not last:
                    rstd(lambda: c.pair(s_x2, 1), mv1, ve1, rs1, s_xv, s_xs, lambda: c.pair(s_xv, 1),
                         c.hold)
                if not first:
                    finish(c, -1)

            run_pairs(pool, pair_work)
            c = Counts(pool, PAIRS - 1)
            finish(c, 0)

            pool.wait_ge(s_gv, 5)

            def add_expert(c, n, e):
                k = n * E + e
                row = c.i * (2 * FG) + (n * FG + FV)
                c.at_least(s_fh, 2 * E, k + 1)
                c.at_least(s_fx, 2 * E, k - 2 + 1)
                pool.tensor_tensor(gated[:, e % 2, :], gl[:, k % 4, :],
                                   gates[:, bass.ds(row, 1), e].to_broadcast([128, T]), ALU.mult)\
                    .then_inc(s_fm, 1)
                if e == 0:
                    c.at_least(s_fT, 2, n - 1)
                c.at_least(s_fm, 2 * E, k + 1)
                c.at_least(s_fx, 2 * E, k)
                before = attn_all[:, :, bass.ds(row, 1)].rearrange("p t b -> p (t b)") if e == 0 \
                    else acc[:, n, FV, :]
                pool.tensor_tensor(acc[:, n, FV, :], gated[:, e % 2, :], before, ALU.add).then_inc(s_fx, 1)

            def tiles(c, first, last):
                for n in range(2):
                    for e in range(E):
                        add_expert(c, n, e)

            run_tiles(pool, tiles)

        @block.scalar
        def _(act):
            act.dma_start(wf[:, :, :], w_gates).then_inc(s_w, 16)
            act.dma_start(bi[:, :, :], b_ih).then_inc(s_w, 16)
            act.dma_start(bh[:, :, :], b_hh).then_inc(s_w, 16)
            act.dma_start(bo[:, :], b_out).then_inc(s_w, 16)
            act.dma_start(xa[:, :], x_tb[0:128, :]).then_inc(s_xa, 16)
            for k in range(KSTEPS + 1):
                if k < KSTEPS:
                    p, rows = k % 2, slice(k * KG, (k + 1) * KG)
                    act.wait_ge(s_kvp, 3 * k + 1)
                    act.activation(kst[:, rows, 0:S], bank[p][:, 0:KG * S].rearrange("p (b s) -> p b s", b=KG),
                                   ACT.Copy, scale=0.5).then_inc(s_kvh, 1)
                    act.wait_ge(s_kvp, 3 * k + 2)
                    if k >= 2:
                        act.wait_ge(s_kvr, 3 * (k - 1))
                    act.copy(v0hi[:, p, :, :], bank[2 + p][:, :].rearrange("p (b j) -> p b j", b=KG))\
                        .then_inc(s_kvh, 1)
                    act.wait_ge(s_kvp, 3 * k + 3)
                    act.copy(v1hi[:, p, :, :], bank[4 + p][:, :].rearrange("p (b j) -> p b j", b=KG))\
                        .then_inc(s_kvh, 1)
                if k >= 1:
                    p, rows = (k - 1) % 2, slice((k - 1) * KG, k * KG)
                    act.wait_ge(s_kvr, 3 * k)
                    if k >= 3:
                        act.wait_ge(s_vl, k - 2)
                    act.copy(kst[:, rows, S:2 * S], kr[:, p, :, :])
                    act.copy(v1mid[:, p, :, :], v1r[:, p, :, :]).then_inc(s_kvm, 1)
            act.wait_ge(s_xT, 1)

            def x_hi(u):
                cols = slice(u * B, (u + 1) * B)
                act.copy(xq[:, 0, cols], ps_xT[:, cols]).then_inc(s_xh, 1)

            x_hi(0)
            act.wait_ge(s_xl, 1)
            x_hi(1)

            def gates(c, k, g):
                c.turn(s_gates, k)
                act.activation(tg[g][:, :, :], ps_gates[g], ACT.Tanh).then_inc(s_tg, 1)
                c.turn(s_c, k)
                act.activation(tc[g][:, :], c2[g][:, :], ACT.Tanh, scale=0.5).then_inc(s_tc, 1)

            def exps(c, k, g):
                c.turn(s_mx, k)
                act.activation(expo[g][:, :], ps_row[g], ACT.Exp, bias=neg_max[g][:, 0:1],
                               accum_out=ps_den[g]).then_inc(s_ex, 1)

            def attn(c, k, g, u):
                c.turn(s_vs, k)
                act.activation(atq[g][:, 0, :], at_in[g][:, :], ACT.Tanh, bias=bo[:, 0:1])
                c.pair(s_yT, -1)
                act.activation(attn_out(u, g), at_in[g][:, :], ACT.Tanh, bias=bo[:, 0:1])\
                    .then_inc(s_at, 1)

            def save_attn(c, k):
                c.turn(s_at, TURNS * (k + 1) - 1)
                i = c.i
                act.copy(attn_all[:, bass.ds((i + k) * U, U), :].rearrange("p u b -> p (u b)"), at[:, :])

            def store_z(c, k):
                c.pair(s_zT, k)
                i = c.i
                dst = zT[:, :, bass.ds((i + k) * U, U)].rearrange("p b u -> p u b")
                act.copy(dst, ps_zT.rearrange("p (u b) -> p u b", u=U)).then_inc(s_zc, 1)

            def pair_work(c, first, last):
                for u in range(U):
                    for g in range(G):
                        gates(c, u * G + g, g)
                    if u == 0 and not first:
                        save_attn(c, -1)
                    for g in range(G):
                        exps(c, u * G + g, g)
                    attn(c, u * G, 0, u)
                    if not last:
                        c.step(s_xg, u)
                        c.pair(s_xT, 1)
                        c.step(s_xl, U - 1 + u)
                        x_hi(u)
                    if u == 1 and not first:
                        store_z(c, -1)
                    for g in range(1, G):
                        attn(c, u * G + g, g, u)

            run_pairs(act, pair_work)
            save_attn(Counts(act, PAIRS - 1), 0)
            store_z(Counts(act, PAIRS - 1), 0)

            act.wait_ge(s_gv, 3)
            act.activation(ge[:, :], lg[:, :], ACT.Exp, bias=ntop[:, 0:1]).then_inc(s_ga, 1)

            def tiles(c, first, last):
                for n in range(2 * E):
                    c.at_least(s_fp, 2 * E, n + 1)
                    for_vector, for_pool = bank[n % 4][:, 0:FV * T], bank[n % 4][:, FV * T:]
                    c.at_least(s_fm, 2 * E, n - 4 + 1)
                    act.activation(gl[:, n % 4, :], for_pool, ACT.Gelu, bias=eb[:, n % E:n % E + 1])\
                        .then_inc(s_fh, 1)
                    act.activation(for_vector, for_vector, ACT.Gelu, bias=eb[:, n % E:n % E + 1]).then_inc(s_fg, 1)

            run_tiles(act, tiles)

        @block.vector
        def _(dve):
            dve.memset(ones[:, :], 1.0).then_inc(s_ms, 1)
            dve.memset(onesf[:, :], 1.0)
            for g in range(G):
                dve.memset(c2[g][:, :], 0.0)
                dve.memset(hq[g][:, :, :], 0.0)
                dve.memset(atq[g][:, :, :], 0.0)
                if g < G - 1:
                    dve.memset(alpha[g][:, :], 0.0)
            dve.memset(alpha[G - 1][:, :], 0.0).then_inc(s_ms, 1)

            dve.wait_ge(s_w, 16 * 7)
            for kind, blocks, factor in ((0, (0, 1, 3), 0.5), (1, (0, 1, 3), 0.5),
                                         (2, (0, 1, 3), 0.25), (2, (2,), 0.5), (3, (0,), 0.5)):
                for m in blocks:
                    w = wf[:, 4 * kind + m, :]
                    dve.tensor_scalar(w, w, factor, None, ALU.mult).then_inc(s_ws, 1)
            dve.tensor_tensor(bi[:, :, :], bi[:, :, :], bh[:, :, :], ALU.add).then_inc(s_b, 1)
            dve.wait_ge(s_b, 1)
            for m in (0, 1, 3):
                dve.tensor_scalar(bi[:, m, :], bi[:, m, :], 0.5, None, ALU.mult).then_inc(s_b, 1)
            dve.wait_ge(s_ws, 11)
            dve.tensor_copy(w3[:, 0, :, :], wf[:, :, :]).then_inc(s_wh, 1)
            dve.wait_ge(s_b, 4)
            dve.tensor_copy(bhi[:, :, :], bi[:, :, :]).then_inc(s_b, 1)
            dve.wait_ge(s_wh, 1)
            dve.tensor_tensor(wf[:, :, :], wf[:, :, :], w3[:, 0, :, :], ALU.subtract).then_inc(s_wr, 1)
            dve.wait_ge(s_b, 5)
            dve.scalar_tensor_tensor(out=bh[:, :, :], in0=bhi[:, :, :], scalar=mask(3), in1=bi[:, :, :],
                                     op0=ALU.mult, op1=ALU.add).then_inc(s_b, 1)
            dve.wait_ge(s_wr, 1)
            dve.tensor_copy(w3[:, 1, :, :], wf[:, :, :]).then_inc(s_wm, 1)
            dve.wait_ge(s_b, 6)
            dve.tensor_copy(bhi[:, :, :], bh[:, :, :]).then_inc(s_b, 1)
            dve.wait_ge(s_wm, 1)
            dve.tensor_tensor(w3[:, 2, :, :], wf[:, :, :], w3[:, 1, :, :], ALU.subtract).then_inc(s_wl, 1)
            dve.wait_ge(s_b, 7)
            dve.scalar_tensor_tensor(out=b3[:, :, :], in0=bhi[:, :, :], scalar=mask(4), in1=bh[:, :, :],
                                     op0=ALU.mult, op1=ALU.add).then_inc(s_wl, 1)

            def ln1_apply(wait_rstd, wait_xn_read):
                wait_rstd()
                wait_xn_read()
                dve.tensor_scalar(xn[:, :], xa[:, :], mv1[:, 0:1], rs1[:, 0:1], ALU.subtract, ALU.mult)\
                    .then_inc(s_xn, 1)

            def x_parts(c, k, u):
                cols = slice(u * B, (u + 1) * B)
                c.step(s_xh, k)
                dve.tensor_tensor(xr[:, cols], ps_xT[:, cols], xq[:, 0, cols], ALU.subtract)
                dve.tensor_tensor(xq[:, 1, cols], ps_xT[:, cols], xq[:, 0, cols], ALU.subtract).then_inc(s_xm, 1)
                c.step(s_xm, k)
                dve.tensor_tensor(xq[:, 2, cols], xr[:, cols], xq[:, 1, cols], ALU.subtract).then_inc(s_xl, 1)

            dve.wait_ge(s_xa, 16)
            dve.bn_stats(st1[:, :], xa[:, :]).then_inc(s_x1, 1)
            dve.wait_ge(s_x1, 1)
            dve.bn_aggr(mv1[:, :], st1[:, :]).then_inc(s_x2, 1)
            ln1_apply(lambda: dve.wait_ge(s_xs, 1), lambda: None)

            for k in range(KSTEPS + 1):
                if k < KSTEPS:
                    p, rows = k % 2, slice(k * KG, (k + 1) * KG)
                    dve.wait_ge(s_kvh, 3 * k + 1)
                    if k >= 2:
                        dve.wait_ge(s_kl, k - 1)
                    dve.scalar_tensor_tensor(
                        out=kr[:, p, :, :], in0=bank[p][:, 0:KG * S].rearrange("p (b s) -> p b s", b=KG),
                        scalar=0.5, in1=kst[:, rows, 0:S], op0=ALU.mult, op1=ALU.subtract).then_inc(s_kvr, 1)
                    dve.wait_ge(s_kvh, 3 * k + 2)
                    dve.scalar_tensor_tensor(
                        out=vst[:, rows, 0, :], in0=v0hi[:, p, :, :], scalar=mask(0),
                        in1=bank[2 + p][:, :].rearrange("p (b j) -> p b j", b=KG),
                        op0=ALU.mult, op1=ALU.add).then_inc(s_kvr, 1)
                    dve.wait_ge(s_kvh, 3 * k + 3)
                    if k >= 2:
                        dve.wait_ge(s_vl, k - 1)
                    dve.scalar_tensor_tensor(
                        out=v1r[:, p, :, :], in0=v1hi[:, p, :, :], scalar=mask(1),
                        in1=bank[4 + p][:, :].rearrange("p (b j) -> p b j", b=KG),
                        op0=ALU.mult, op1=ALU.add).then_inc(s_kvr, 1)
                if k >= 1:
                    p, rows = (k - 1) % 2, slice((k - 1) * KG, k * KG)
                    dve.wait_ge(s_kvm, k)
                    dve.scalar_tensor_tensor(
                        out=vst[:, rows, 1, :], in0=v1mid[:, p, :, :], scalar=mask(2), in1=v1r[:, p, :, :],
                        op0=ALU.mult, op1=ALU.add).then_inc(s_vl, 1)
            for u in range(U):
                x_parts(Counts(dve, 0), u, u)

            def cell(c, k, g):
                t_in, t_forget, t_cell, t_out = (tg[g][:, m, :] for m in range(4))
                c.turn(s_tg, k)
                dve.scalar_tensor_tensor(out=in_term[g][:, :], in0=t_in, scalar=1.0, in1=t_cell,
                                         op0=ALU.add, op1=ALU.mult)
                dve.scalar_tensor_tensor(out=forget_term[g][:, :], in0=t_forget, scalar=1.0, in1=c2[g][:, :],
                                         op0=ALU.add, op1=ALU.mult).then_inc(s_ct, 1)
                c.turn(s_ct, k)
                dve.scalar_tensor_tensor(out=c2[g][:, :], in0=forget_term[g][:, :], scalar=0.5,
                                         in1=in_term[g][:, :], op0=ALU.mult, op1=ALU.add).then_inc(s_c, 1)
                c.turn(s_tc, k)
                dve.scalar_tensor_tensor(out=hq[g][:, 0, :], in0=t_out, scalar=1.0, in1=tc[g][:, :],
                                         op0=ALU.add, op1=ALU.mult)
                dve.scalar_tensor_tensor(out=h2[g][:, :], in0=t_out, scalar=1.0, in1=tc[g][:, :],
                                         op0=ALU.add, op1=ALU.mult).then_inc(s_h, 1)
                c.turn(s_h, k)
                dve.tensor_tensor(hr[g][:, :], h2[g][:, :], hq[g][:, 0, :], ALU.subtract)
                dve.tensor_tensor(hq[g][:, 1, :], h2[g][:, :], hq[g][:, 0, :], ALU.subtract).then_inc(s_hm, 1)
                c.turn(s_hm, k)
                dve.tensor_tensor(hq[g][:, 2, :], hr[g][:, :], hq[g][:, 1, :], ALU.subtract).then_inc(s_hl, 1)

            def score_sum(c, k, g):
                c.turn(s_sp, k)
                dve.tensor_reduce(sc[g][:, :, :], ps_sc[g], AX_X, ALU.add).then_inc(s_ss, 1)

            def row_max(c, k, g):
                c.turn(s_row, k)
                dve.tensor_reduce(neg_max[g][:, :], ps_row[g], AX_X, ALU.max, negate=True).then_inc(s_mx, 1)

            def normalise(c, k, g):
                c.turn(s_ex, k)
                dve.reciprocal(rden[g][:, :], ps_den[g]).then_inc(s_rd, 1)
                c.turn(s_rd, k)
                for first, count in ((0, SA), (SA, SB)):
                    last = dve.tensor_scalar(
                        alpha[g][:, Q * first:Q * (first + count)].rearrange("p (k s) -> p k s", k=Q),
                        expo[g][:, first:first + count].unsqueeze(1).to_broadcast([NB, Q, count]),
                        rden[g][:, 0:1], None, ALU.mult)
                last.then_inc(s_al, 1)

            def alpha_parts(c, k, g):
                c.turn(s_aT, k)
                dve.tensor_copy(aq[g][:, 0, :, :], ps_alT[g]).then_inc(s_ah, 1)
                c.turn(s_ah, k)
                dve.tensor_tensor(ar[g][:, :, :], ps_alT[g], aq[g][:, 0, :, :], ALU.subtract)
                dve.tensor_tensor(aq[g][:, 1, :, :], ps_alT[g], aq[g][:, 0, :, :], ALU.subtract)\
                    .then_inc(s_am, 1)
                c.turn(s_am, k)
                dve.tensor_tensor(aq[g][:, 2, :, :], ar[g][:, :, :], aq[g][:, 1, :, :], ALU.subtract)\
                    .then_inc(s_as, 1)

            def value_sum(c, k, g):
                c.turn(s_vp, k)
                dve.tensor_reduce(at_in[g][:, :], ps_val[g], AX_X, ALU.add).then_inc(s_vs, 1)

            def attn_parts(c, k, g, u):
                c.turn(s_at, k)
                dve.tensor_tensor(at_r[g][:, :], attn_out(u, g), atq[g][:, 0, :], ALU.subtract)
                dve.tensor_tensor(atq[g][:, 1, :], attn_out(u, g), atq[g][:, 0, :], ALU.subtract)\
                    .then_inc(s_tm, 1)
                c.turn(s_tm, k)
                dve.tensor_tensor(atq[g][:, 2, :], at_r[g][:, :], atq[g][:, 1, :], ALU.subtract)\
                    .then_inc(s_ts, 1)

            def ln2_add(c, k):
                c.pair(s_yT, k)
                c.pair(s_xb, k, 16)
                dve.tensor_tensor(y[:, :], ps_y, xb[:, :], ALU.add).then_inc(s_y, 1)

            def ln2_stats(c, k):
                c.pair(s_y, k)
                dve.bn_stats(st2[:, :], y[:, :]).then_inc(s_y1, 1)

            def ln2_mean_var(c, k):
                c.pair(s_y1, k)
                c.hold()
                dve.bn_aggr(mv2[:, :], st2[:, :]).then_inc(s_y2, 1)

            def ln2_apply(c, k):
                c.pair(s_ys, k)
                dve.tensor_scalar(z[:, :], y[:, :], mv2[:, 0:1], rs2[:, 0:1], ALU.subtract, ALU.mult)\
                    .then_inc(s_z, 1)

            def pair_work(c, first, last):
                for u in range(U):
                    k0, k1 = u * G, u * G + 1
                    ln1, ln2 = (u == 0 and not last), (u == 1 and not first)
                    cell(c, k0, 0)
                    cell(c, k1, 1)
                    score_sum(c, k0, 0)
                    if ln1:
                        c.pair(s_xa, 1, 16)
                        dve.bn_stats(st1[:, :], xa[:, :]).then_inc(s_x1, 1)
                    if ln2:
                        ln2_add(c, -1)
                    row_max(c, k0, 0)
                    if ln1:
                        c.pair(s_x1, 1)
                        c.hold()
                        dve.bn_aggr(mv1[:, :], st1[:, :]).then_inc(s_x2, 1)
                    if ln2:
                        ln2_stats(c, -1)
                    normalise(c, k0, 0)
                    if ln1:
                        ln1_apply(lambda: c.pair(s_xs, 1), lambda: c.pair(s_xT, 0))
                    if ln2:
                        ln2_mean_var(c, -1)
                    score_sum(c, k1, 1)
                    alpha_parts(c, k0, 0)
                    row_max(c, k1, 1)
                    normalise(c, k1, 1)
                    if ln2:
                        ln2_apply(c, -1)
                    alpha_parts(c, k1, 1)
                    value_sum(c, k0, 0)
                    attn_parts(c, k0, 0, u)
                    if not last:
                        x_parts(c, U + u, u)
                    value_sum(c, k1, 1)
                    attn_parts(c, k1, 1, u)

            run_pairs(dve, pair_work)
            c = Counts(dve, PAIRS - 1)
            ln2_add(c, 0)
            ln2_stats(c, 0)
            ln2_mean_var(c, 0)
            ln2_apply(c, 0)

            dve.wait_ge(s_gt, 1)
            dve.tensor_copy(pooled[:, :], bank[4][:, 0:B]).then_inc(s_gv, 1)
            dve.wait_ge(s_gt, 2)
            dve.wait_ge(s_ew, 64)
            dve.tensor_tensor(lg[:, :], bank[4][0:B, B:B + E], gb[:, :], ALU.add).then_inc(s_gv, 1)
            dve.wait_ge(s_gv, 2)
            dve.max(top[:, :], lg[:, :]).then_inc(s_b, 1)
            dve.wait_ge(s_b, 8)
            dve.tensor_scalar(ntop[:, :], top[:, 0:1], -1.0, None, ALU.mult).then_inc(s_gv, 1)
            dve.tensor_scalar(keep[:, :], lg[:, :], top[:, 1:2], None, ALU.is_ge).then_inc(s_b, 1)
            dve.wait_ge(s_ga, 1)
            dve.wait_ge(s_b, 9)
            dve.tensor_tensor(gk[:, :], ge[:, :], keep[:, :], ALU.mult).then_inc(s_b, 1)
            dve.wait_ge(s_b, 10)
            dve.tensor_reduce(gs[:, :], gk[:, :], AX_X, ALU.add).then_inc(s_b, 1)
            dve.wait_ge(s_b, 11)
            dve.reciprocal(gr[:, :], gs[:, :]).then_inc(s_b, 1)
            dve.wait_ge(s_b, 12)
            dve.tensor_scalar(ge[:, :], gk[:, :], gr[:, 0:1], None, ALU.mult).then_inc(s_b, 1)
            dve.wait_ge(s_b, 13)
            dve.tensor_tensor(gd[:, :, :], ge[:, :].unsqueeze(1).to_broadcast([B, B, E]),
                              cst[0:B, C_ID:C_ID + B].unsqueeze(2).to_broadcast([B, B, E]), ALU.mult)\
                .then_inc(s_gv, 1)
            dve.wait_ge(s_gt, 3)
            dve.tensor_copy(gates[:, :, :], bank[5][:, :].rearrange("p (b e) -> p b e", e=E)).then_inc(s_gv, 1)
            dve.wait_ge(s_gv, 5)

            def add_expert(c, n, e):
                c.at_least(s_fg, 2 * E, n * E + e + 1)
                if e == 0:
                    c.at_least(s_fT, 2, n - 1)
                for j in range(FV):
                    c.at_least(s_fv, 2 * E * FV, (n * E + e - 1) * FV + j + 1)
                    q = j
                    row = c.i * (2 * FG) + (n * FG + q)
                    before = attn_all[:, :, bass.ds(row, 1)].rearrange("p t b -> p b t") if e == 0 \
                        else acc[:, n, q:q + 1, :]
                    dve.scalar_tensor_tensor(
                        out=acc[:, n, q:q + 1, :],
                        in0=bank[(n * E + e) % 4][:, q * T:(q + 1) * T].unsqueeze(1),
                        scalar=gates[:, bass.ds(row, 1), e], in1=before, op0=ALU.mult, op1=ALU.add)\
                        .then_inc(s_fv, 1)

            def result(c, n, ago):
                p, back = (n - ago) % 2, (1 if ago > n else 0)
                c.at_least(s_fT, 2, n - ago + 1)
                c.at_least(s_xo[p], 16, 16 * (1 - back))
                dve.tensor_tensor(res[:, p, :, :], bank[6 + p][:, :].rearrange("p (b d) -> p b d", b=FG),
                                  xo[:, p, :, :], ALU.add).then_inc(s_fr, 1)

            def tiles(c, first, last):
                for n in range(2):
                    for e in range(E):
                        add_expert(c, n, e)
                        if e == 5 and not (first and n == 0):
                            result(c, n, 1)
                if last:
                    result(c, 1, 0)

            run_tiles(dve, tiles)

        @block.tensor
        def _(pe):
            mm = pe.matmul
            pe.wait_ge(s_w, 16 * 7)
            for k in range(KSTEPS):
                p = k % 2
                if k % (KSTEPS // 4) == 0:
                    pe.wait_ge(s_ctx[k // (KSTEPS // 4)], 16)
                def reusable(product):
                    if k >= 2:
                        pe.wait_ge(s_kvr, 3 * (k - 2) + product + 1)

                reusable(0)
                mm(bank[p][:, 0:KG * S], wq[:, :], ctxT[:, k * KG:(k + 1) * KG, 0:S], start=True, stop=True)\
                    .then_inc(s_kvp, 1)
                reusable(1)
                for q in range(KG):
                    for half in range(2):
                        last = mm(bank[2 + p][half * SA:(half + 1) * SA, q * 128:(q + 1) * 128],
                                  ctxT[:, k * KG + q, 0:SA], wo[:, :], start=True, stop=True)
                last.then_inc(s_kvp, 1)
                reusable(2)
                for q in range(KG):
                    last = mm(bank[4 + p][:, q * 128:(q + 1) * 128], ctxT[:, k * KG + q, :], wo[:, :],
                              start=True, stop=True)
                last.then_inc(s_kvp, 1)
            pe.wait_ge(s_kvr, 3 * KSTEPS)
            pe.wait_ge(s_xn, 1)
            pe.transpose(ps_xT, xn[:, :], ident).then_inc(s_xT, 1)

            def h_gates(g, products):
                for m in range(4):
                    for wp, hp in products:
                        mm(ps_gates[g][:, m, :], w3[:, wp, 8 + m, :], hq[g][:, hp, :],
                           start=(m == 0 and (wp, hp) == PRODUCTS[0]), stop=False, skip_group_check=True)

            def x_gates(g, u):
                for m in range(4):
                    o = ps_gates[g][:, m, :]
                    mm(o, b3[:, m, :], ones[:, 0:NB], start=False, stop=False, skip_group_check=True)
                    for wp, xp in PRODUCTS:
                        cols = slice(u * B + g * NB, u * B + (g + 1) * NB)
                        last = mm(o, w3[:, wp, m, :], xq[:, xp, cols], start=False, stop=False,
                                  skip_group_check=True)
                if g == G - 1:
                    last.then_inc(s_xg, 1)

            def attn_gates(c, k, g):
                c.turn(s_ts, k - G)
                o = ps_gates[g]
                for m in range(4):
                    for wp, ap in PRODUCTS:
                        last = mm(o[:, m, :], w3[:, wp, 4 + m, :], atq[g][:, ap, :], start=False,
                                  stop=(wp, ap) == PRODUCTS[-1], skip_group_check=True)
                last.then_inc(s_gates, 1)

            def scores(c, k, g):
                c.turn(s_hl, k)
                for j in range(NB):
                    for pack in range(2):
                        last = mm(ps_sc[g][:, pack, j, :], kst[:, g * NB + j, pack * 128:(pack + 1) * 128],
                                  hq[g][:, :, j], start=True, stop=True)
                last.then_inc(s_sp, 1)

            def h_out(g, opens):
                for n, (wp, hp) in enumerate(PRODUCTS):
                    mm(ps_val[g][:, :, 0], w3[:, wp, 12, :], hq[g][:, hp, :], start=(opens and n == 0),
                       stop=False, skip_group_check=True)

            def rows(c, k, g):
                c.turn(s_ss, k)
                for pack in range(2):
                    last = mm(ps_row[g], sc[g][:, pack, :], sel(pack), start=(pack == 0), stop=(pack == 1))
                last.then_inc(s_row, 1)

            def turn_alpha(c, k, g):
                c.turn(s_al, k)
                c.hold()
                id_nb = cst[0:NB, C_ID:C_ID + NB]
                for pack in range(2):
                    last = pe.transpose(ps_alT[g][:, pack, :], alpha[g][:, pack * 128:(pack + 1) * 128], id_nb)
                last.then_inc(s_aT, 1)

            def values(c, k, g, rows_):
                c.turn(s_as, k)
                for j in rows_:
                    for pack in range(2):
                        last = mm(ps_val[g][:, j, :], vst[:, g * NB + j, pack, :], aq[g][:, :, pack, j],
                                  start=False, stop=(pack == 1), skip_group_check=True)
                if rows_[-1] == NB - 1:
                    last.then_inc(s_vp, 1)

            pe.wait_ge(s_wl, 2)
            pe.wait_ge(s_xl, U)
            pe.wait_ge(s_ms, 2)
            pe.wait_ge(s_kc, 1)
            pe.wait_ge(s_kl, KSTEPS)
            pe.wait_ge(s_vl, KSTEPS)
            h_gates(0, PRODUCTS)
            x_gates(0, 0)
            cut = 3 * NB // 4

            def pair_work(c, first, last):
                for u in range(U):
                    last_step = last and u == U - 1
                    k0, k1 = u * G, u * G + 1
                    attn_gates(c, k0, 0)
                    c.turn(s_vs, k1 - G)
                    h_gates(1, PRODUCTS)
                    x_gates(1, u)
                    attn_gates(c, k1, 1)
                    if u == 0 and not first:
                        pe.transpose(ps_y, at[:, :], ident).then_inc(s_yT, 1)
                    if not last_step:
                        c.turn(s_h, k0)
                        h_gates(0, WITH_HI)
                    scores(c, k0, 0)
                    if not last_step:
                        h_gates(0, WITHOUT_HI)
                    h_out(0, last_step)
                    rows(c, k0, 0)
                    scores(c, k1, 1)
                    turn_alpha(c, k0, 0)
                    h_out(1, False)
                    if u == 0 and not last:
                        c.pair(s_xn, 1)
                        c.step(s_xl, U - 1)
                        pe.transpose(ps_xT, xn[:, :], ident).then_inc(s_xT, 1)
                    rows(c, k1, 1)
                    values(c, k0, 0, range(cut))
                    turn_alpha(c, k1, 1)
                    if u == 1 and not first:
                        c.pair(s_z, -1)
                        pe.transpose(ps_zT, z[:, :], ident).then_inc(s_zT, 1)
                    if not last_step:
                        c.step(s_xl, u + 1)
                        x_gates(0, 1 - u)
                    values(c, k0, 0, range(cut, NB))
                    values(c, k1, 1, range(NB))

            run_pairs(pe, pair_work)
            c = Counts(pe, PAIRS - 1)
            for g in range(G):
                c.turn(s_at, TURNS - G + g)
            c.pair(s_y, -1)
            pe.transpose(ps_y, at[:, :], ident).then_inc(s_yT, 1)
            c.pair(s_z, 0)
            c.pair(s_zc, -1)
            pe.transpose(ps_zT, z[:, :], ident).then_inc(s_zT, 1)

            pe.wait_ge(s_zs, PAIRS + 1)
            pe.wait_ge(s_ew, 64)
            mm(bank[4][:, 0:B], zsum[:, :], fold, start=True, stop=True).then_inc(s_gt, 1)
            pe.wait_ge(s_gv, 1)
            mm(bank[4][0:B, B:B + E], pooled[:, :], gw[:, :], start=True, stop=True).then_inc(s_gt, 1)
            pe.wait_ge(s_gv, 4)
            mm(bank[5][:, :], onesf[:, :], gd[:, :, :].rearrange("p b e -> p (b e)"), start=True, stop=True)\
                .then_inc(s_gt, 1)
            pe.wait_ge(s_zc, PAIRS)

            def tile_back(c, n, ago):
                p = (n - ago) % 2
                c.at_least(s_fv, 2 * E * FV, (n - ago + 1) * E * FV)
                c.at_least(s_fx, 2 * E, (n - ago + 1) * E)
                for q in range(FG):
                    last = pe.transpose(bank[6 + p][:, q * 128:(q + 1) * 128], acc[:, p, q, :], ident)
                last.then_inc(s_fT, 1)

            def tiles(c, first, last):
                for n in range(2):
                    for e in range(E):
                        k = n * E + e
                        c.at_least(s_fv, 2 * E * FV, (k - 4 + 1) * FV)
                        pe.matmul(bank[k % 4][:, :], ew[:, e, :],
                                  zT[:, bass.ds(c.i * (2 * FG) + n * FG, FG), :].rearrange("p b t -> p (b t)"),
                                  start=True, stop=True).then_inc(s_fp, 1)
                        if e == 4 and not (first and n == 0):
                            tile_back(c, n, 1)
                if last:
                    tile_back(c, 1, 0)

            run_tiles(pe, tiles)


def kernel(x, ctx_1024, L0_xattn_W_ih, L0_xattn_W_hh, L0_xattn_b_ih, L0_xattn_b_hh, L0_xattn_Wq,
           L0_xattn_Wout, L0_xattn_b_out, L0_ffn_gate_w, L0_ffn_gate_b, L0_ffn_expert_w, L0_ffn_expert_b):
    import concourse.bacc as bacc
    from concourse.bass_utils import run_bass_kernel_spmd as run

    x, context = np.asarray(x), np.asarray(ctx_1024)
    w_ih, w_hh, w_out = (np.asarray(a) for a in (L0_xattn_W_ih, L0_xattn_W_hh, L0_xattn_Wout))
    c_t = context.transpose(2, 0, 1)
    ctx_dup = np.zeros((D, B, 128), np.float32)
    ctx_dup[:, :, :S] = c_t
    for k in (1, 2):
        ctx_dup[:, :, SA + k * SB:SA + (k + 1) * SB] = c_t[:, :, SA:]
    w_gates = np.concatenate([w_ih[:, :D].T, w_ih[:, D:].T, w_hh.T, w_out[:, D:].T], axis=1)

    def bias_rows(b):
        rows = np.zeros((128, 4 * 128), np.float32)
        rows[[0, 32, 64]] = np.asarray(b)
        return rows.reshape(128, 4, 128)

    arrays = {
        "x_tbd": x.transpose(1, 0, 2),
        "ctx_dup": ctx_dup,
        "w_gates": w_gates.reshape(128, 13, 128),
        "b_ih": bias_rows(L0_xattn_b_ih),
        "b_hh": bias_rows(L0_xattn_b_hh),
        "w_q": np.asarray(L0_xattn_Wq),
        "w_out": w_out[:, :D].T,
        "b_out": np.asarray(L0_xattn_b_out).reshape(128, 1),
        "gate_w": np.asarray(L0_ffn_gate_w).T,
        "gate_b": np.repeat(np.asarray(L0_ffn_gate_b)[None, :], B, axis=0),
        "expert_w": np.asarray(L0_ffn_expert_w).transpose(2, 0, 1),
        "expert_b": np.asarray(L0_ffn_expert_b).T,
        "consts": constants(),
    }
    arrays = {k: np.ascontiguousarray(v) for k, v in arrays.items()}
    nc = bacc.Bacc("TRN2", target_bir_lowering=False, num_devices=1)
    ins = {k: nc.dram_tensor(f"in_{k}", v.shape, mybir.dt.from_np(v.dtype), kind="ExternalInput").ap()
           for k, v in arrays.items()}
    out = nc.dram_tensor("out", (T, B, D), F32, kind="ExternalOutput").ap()
    xattn_moe(nc, **ins, out=out)
    got = run(nc, [{f"in_{k}": v for k, v in arrays.items()}], core_ids=[0]).results[0]["out"]
    return np.ascontiguousarray(np.asarray(got).transpose(1, 0, 2))
```

```python
from contextlib import ExitStack

import numpy as np

import concourse.bass as bass
from concourse import mybir

ALU = mybir.AluOpType
ACT = mybir.ActivationFunctionType
AX_X = mybir.AxisListType.X
F32 = mybir.dt.float32
BF16 = mybir.dt.bfloat16

B, T, D, S, E = 64, 128, 128, 77, 8
H = D
EPS = 1e-5
G = 2
NB = B // G
U = 2
PAIRS = T // U
TURNS = U * G
Q = 3
SA = 64
SB = S - SA
SD = SA + Q * SB
PRODUCTS = ((2, 0), (1, 1), (0, 2), (1, 0), (0, 1), (0, 0))
WITH_HI = tuple(p for p in PRODUCTS if p[1] == 0)
WITH_MID = tuple(p for p in PRODUCTS if p[1] == 1)
WITH_LO = tuple(p for p in PRODUCTS if p[1] == 2)
KG = 4
KSTEPS = B // KG
FG = 4
FTILES = B // FG
FV = FG - 1

C_ID = 0
C_SEL = C_ID + 128
C_FOLD = C_SEL + 2 * S
C_MASK = C_FOLD + B
C_ALL = C_MASK + 5


WEIGHT_FACTORS = ((0, 2, 0.5), (3, 3, 0.5), (7, 1, 0.5), (8, 2, 0.25), (10, 1, 0.5), (11, 1, 0.25), (12, 1, 0.5))


def constants():
    c = np.zeros((128, C_ALL), np.float32)
    c[:, C_ID:C_ID + 128] = np.eye(128)
    for col in range(Q * S):
        c[col % 128, C_SEL + (col // 128) * S + col % S] = 1
    for r in range(128):
        c[r, C_FOLD + r % B] = 1.0 / T
    c[SA:, C_MASK + 0] = -1
    c[:SA, C_MASK + 1] = -1
    c[SA + SB:, C_MASK + 1] = -1
    c[:SA, C_MASK + 2] = -1
    c[SA + 2 * SB:, C_MASK + 2] = -1
    c[32:, C_MASK + 3] = -1
    c[64:, C_MASK + 4] = -1
    return c


def xattn_moe(nc, x_tbd, ctx_dup, w_gates, b_ih, b_hh, w_q, w_out, b_out,
              gate_w, gate_b, expert_w, expert_b, consts, out):
    x_tb = x_tbd.rearrange("t b d -> (t b) d")
    with ExitStack() as ctx:
        def sb(name, shape, dt):
            return ctx.enter_context(nc.sbuf_tensor(name, shape, dt))

        def sem(name):
            return ctx.enter_context(nc.semaphore(name))

        cst = sb("cst", [128, C_ALL], F32)
        ident = cst[:, C_ID:C_ID + 128]
        fold = cst[:, C_FOLD:C_FOLD + B]

        def sel(pack):
            return cst[:, C_SEL + pack * S:C_SEL + (pack + 1) * S]

        def mask(n):
            return cst[:, C_MASK + n:C_MASK + n + 1]

        ctx_attn = sb("ctx_attn", [128, B * 128], F32)
        ctxT = ctx_attn[:, :].rearrange("p (b s) -> p b s", b=B)
        attn_all = ctx_attn[:, :].rearrange("p (t b) -> p t b", t=T)
        kst = sb("kst", [128, B, 2 * 128], BF16)
        vst = sb("vst", [128, B, 2, 128], BF16)
        zT = sb("zT", [128, B, T], F32)
        wf = sb("wf", [128, 13, 128], F32)
        w3 = sb("w3", [128, Q, 13, 128], BF16)
        wq = sb("wq", [128, H], F32)
        wo = sb("wo", [128, 128], F32)
        bi = sb("bi", [128, 4, 128], F32)
        bh = sb("bh", [128, 4, 128], F32)
        bhi = sb("bhi", [128, 4, 128], BF16)
        b3 = sb("b3", [128, 4, 128], BF16)
        ones = sb("ones", [128, B], BF16)
        onesf = sb("onesf", [B, 128], F32)
        bo = sb("bo", [128, 1], F32)
        ew = sb("ew", [128, E, 128], F32)
        eb = sb("eb", [128, E], F32)
        gw = sb("gw", [128, E], F32)
        gb = sb("gb", [B, E], F32)
        kr = sb("kr", [128, 2, KG, S], F32)
        v0hi = sb("v0hi", [128, 2, KG, 128], BF16)
        v1hi = sb("v1hi", [128, 2, KG, 128], BF16)
        v1r = sb("v1r", [128, 2, KG, 128], F32)
        v1mid = sb("v1mid", [128, 2, KG, 128], BF16)
        tg = [sb(f"tg{g}", [128, 4, NB], F32) for g in range(G)]
        c2 = [sb(f"c2_{g}", [128, NB], F32) for g in range(G)]
        in_term = [sb(f"in_term{g}", [128, NB], F32) for g in range(G)]
        forget_term = [sb(f"forget_term{g}", [128, NB], F32) for g in range(G)]
        tc = [sb(f"tc{g}", [128, NB], F32) for g in range(G)]
        h2 = [sb(f"h2_{g}", [128, NB], F32) for g in range(G)]
        hr = [sb(f"hr{g}", [128, NB], F32) for g in range(G)]
        hq = [sb(f"hq{g}", [128, Q, NB], BF16) for g in range(G)]
        sc = [sb(f"sc{g}", [128, 2, NB], F32) for g in range(G)]
        neg_max = [sb(f"neg_max{g}", [NB, 1], F32) for g in range(G)]
        expo = [sb(f"expo{g}", [NB, S], F32) for g in range(G)]
        rden = [sb(f"rden{g}", [NB, 1], F32) for g in range(G)]
        alpha = [sb(f"alpha{g}", [NB, 2 * 128], F32) for g in range(G)]
        ar = [sb(f"ar{g}", [128, 2, NB], F32) for g in range(G)]
        aq = [sb(f"aq{g}", [128, Q, 2, NB], BF16) for g in range(G)]
        at_in = [sb(f"at_in{g}", [128, NB], F32) for g in range(G)]
        at_r = [sb(f"at_r{g}", [128, NB], F32) for g in range(G)]
        atq = [sb(f"atq{g}", [128, Q, NB], BF16) for g in range(G)]
        at = sb("at", [128, U * B], F32)
        xa = sb("xa", [128, D], F32)
        xb = sb("xb", [128, D], F32)
        st1 = sb("st1", [128, 6], F32)
        st2 = sb("st2", [128, 6], F32)
        mv1 = sb("mv1", [128, 2], F32)
        mv2 = sb("mv2", [128, 2], F32)
        ve1 = sb("ve1", [128, 1], F32)
        ve2 = sb("ve2", [128, 1], F32)
        rs1 = sb("rs1", [128, 1], F32)
        rs2 = sb("rs2", [128, 1], F32)
        mhalf = sb("mhalf", [128, 1], F32)
        xn = sb("xn", [128, D], F32)
        xq = sb("xq", [128, Q, U * B], BF16)
        xr = sb("xr", [128, U * B], F32)
        y = sb("y", [128, D], F32)
        z = sb("z", [128, D], F32)
        zsum = sb("zsum", [128, D], F32)
        pooled = sb("pooled", [128, B], F32)
        lg = sb("lg", [B, E], F32)
        top = sb("top", [B, 8], F32)
        ntop = sb("ntop", [B, 1], F32)
        keep = sb("keep", [B, E], F32)
        ge = sb("ge", [B, E], F32)
        gk = sb("gk", [B, E], F32)
        gs = sb("gs", [B, 1], F32)
        gr = sb("gr", [B, 1], F32)
        gd = sb("gd", [B, B, E], F32)
        gates = sb("gates", [128, B, E], F32)
        gl = sb("gl", [128, 4, T], F32)
        tile_gates = sb("tile_gates", [128, 2, FG, E], F32)
        gated = sb("gated", [128, 2, T], F32)
        acc = sb("acc", [128, 2, FG, T], F32)
        xo = v1r
        res = sb("res", [128, 2, FG, D], F32)

        bank = [ctx.enter_context(nc.psum_tensor(f"bank{n}", [128, 512], F32)) for n in range(8)]
        ps_gates = [bank[g][:, 0:4 * NB].rearrange("p (m b) -> p m b", m=4) for g in range(G)]
        ps_val = [bank[g][:, 4 * NB:(4 + Q) * NB].rearrange("p (b q) -> p b q", q=Q) for g in range(G)]
        ps_sc = [bank[2 + g][:, 0:2 * NB * Q].rearrange("p (k b q) -> p k b q", k=2, q=Q) for g in range(G)]
        ps_row = [bank[2 + g][0:NB, 256:256 + S] for g in range(G)]
        ps_den = [bank[2 + g][0:NB, 448:449] for g in range(G)]
        ps_alT = [bank[2 + g][:, 384:384 + 2 * NB].rearrange("p (k b) -> p k b", k=2) for g in range(G)]
        ps_xT = bank[7][:, 0:128]
        ps_y = bank[5][:, 0:128]
        ps_zT = bank[6][:, 0:128]

        s_kw = sem("kv_weights_loaded")
        s_bw = sem("biases_loaded")
        s_w = sem("weights_loaded")
        s_ctx = [sem(f"context_loaded{n}") for n in range(4)]
        s_ew = sem("expert_weights_loaded")
        s_ms = sem("memsets_done")
        s_pm = sem("pool_memsets_done")
        s_kc = sem("kst_cleared")
        s_ws = sem("weights_scaled")
        s_wh = sem("weights_hi")
        s_wr = sem("weights_rest")
        s_wm = sem("weights_mid")
        s_wl = sem("weights_split")
        s_b = sem("bias_chain")
        s_kvp = sem("kv_products")
        s_kvh = sem("kv_hi")
        s_kvr = sem("kv_rest")
        s_kvm = sem("kv_mid")
        s_kl = sem("k_lo")
        s_vl = sem("v_lo")
        s_gates = sem("gates_ready")
        s_tg = sem("gates_tanh")
        s_ct = sem("c_terms")
        s_c = sem("c_ready")
        s_tc = sem("c_tanh")
        s_h = sem("h_hi")
        s_hm = sem("h_mid")
        s_hl = sem("h_split")
        s_sp = sem("score_parts")
        s_ss = sem("score_sums")
        s_row = sem("score_rows")
        s_mx = sem("neg_max_ready")
        s_ex = sem("exp_ready")
        s_rd = sem("rden_ready")
        s_al = sem("alpha_ready")
        s_aT = sem("alpha_transposed")
        s_ah = sem("alpha_hi")
        s_am = sem("alpha_mid")
        s_as = sem("alpha_split")
        s_vp = sem("value_parts")
        s_vs = sem("value_sums")
        s_at = sem("attn_ready")
        s_tm = sem("attn_mid")
        s_ts = sem("attn_split")
        s_xa = sem("xa_loaded")
        s_x1 = sem("ln1_stats")
        s_x2 = sem("ln1_mean_var")
        s_xv = sem("ln1_var_eps")
        s_xs = sem("ln1_rstd")
        s_xn = sem("ln1_ready")
        s_xT = sem("ln1_transposed")
        s_xh = sem("x_hi")
        s_xm = sem("x_mid")
        s_xl = sem("x_split")
        s_xg = sem("x_gates_done")
        s_xb = sem("xb_loaded")
        s_yT = sem("attn_pair_transposed")
        s_y = sem("y_ready")
        s_y1 = sem("ln2_stats")
        s_y2 = sem("ln2_mean_var")
        s_yv = sem("ln2_var_eps")
        s_ys = sem("ln2_rstd")
        s_z = sem("z_ready")
        s_zs = sem("z_summed")
        s_zT = sem("z_transposed")
        s_zc = sem("z_stored")
        s_gt = sem("gating_tensor")
        s_gv = sem("gating_vector")
        s_ga = sem("gating_scalar")
        s_fc = sem("tile_gates_ready")
        s_fp = sem("expert_products")
        s_fg = sem("expert_gelu_vector")
        s_fh = sem("expert_gelu_pool")
        s_fv = sem("expert_added_vector")
        s_fm = sem("expert_gated_pool")
        s_fx = sem("expert_added_pool")
        s_fT = sem("tile_transposed")
        s_fr = sem("tile_result")
        s_xo = [sem(f"residual_loaded{n}") for n in range(2)]
        s_held = sem("held")
        s_out = [sem(f"tile_stored{n}") for n in range(2)]

        block = ctx.enter_context(nc.Block())

        class Counts:

            def __init__(self, eng, i):
                self.eng, self.i, self.known, self.ago = eng, i, {}, 0

            def pair_before(self):
                c = Counts(self.eng, self.i)
                c.known, c.ago = self.known, self.ago + 1
                return c

            def at_least(self, s, per_pair, n):
                n -= per_pair * self.ago
                if isinstance(self.i, int):
                    if per_pair * self.i + n > 0:
                        self.eng.wait_ge(s, per_pair * self.i + n)
                    return
                if (per_pair, n) not in self.known:
                    self.known[per_pair, n] = self.eng.snap(self.i * per_pair + n)
                self.eng.wait_ge(s, self.known[per_pair, n])

            def hold(self):
                if not isinstance(self.i, int):
                    self.eng.sem_inc(s_held, 1)

            def turn(self, s, k):
                self.at_least(s, TURNS, k + 1)

            def step(self, s, k):
                self.at_least(s, U, k + 1)

            def pair(self, s, k, by=1):
                self.at_least(s, by, by * (k + 1))

        def run_pairs(eng, body):
            body(Counts(eng, 0), True, False)
            with eng.Fori(1, PAIRS - 1) as i:
                body(Counts(eng, i), False, False)
            body(Counts(eng, PAIRS - 1), False, True)

        def attn_out(u, g):
            return at[:, u * B + g * NB:u * B + (g + 1) * NB]

        def run_pairs_in_two(eng, head, tail):
            head(Counts(eng, 0), True, False)
            with eng.Fori(1, PAIRS - 1) as i:
                c = Counts(eng, i)
                tail(c.pair_before(), False)
                head(c, False, False)
            tail(Counts(eng, PAIRS - 2), False)
            head(Counts(eng, PAIRS - 1), False, True)
            tail(Counts(eng, PAIRS - 1), True)

        def run_tiles(eng, body):
            body(Counts(eng, 0), True, False)
            with eng.Fori(1, FTILES // 2 - 1) as i:
                body(Counts(eng, i), False, False)
            body(Counts(eng, FTILES // 2 - 1), False, True)

        @block.sync
        def _(sp):
            sp.dma_start(wo[:, :], w_out).then_inc(s_kw, 16)
            sp.dma_start(wq[:, :], w_q).then_inc(s_kw, 16)
            sp.dma_start(cst[:, :], consts).then_inc(s_kw, 16)
            for n in range(4):
                part = slice(n * B // 4, (n + 1) * B // 4)
                sp.dma_start(ctxT[:, part, :], ctx_dup[:, part, :]).then_inc(s_ctx[n], 16)
            sp.dma_start(xb[:, :], x_tb[0:128, :]).then_inc(s_xb, 16)
            sp.dma_start(ew[:, :, :], expert_w).then_inc(s_ew, 16)
            sp.dma_start(eb[:, :], expert_b).then_inc(s_ew, 16)
            sp.dma_start(gw[:, :], gate_w).then_inc(s_ew, 16)
            sp.dma_start(gb[:, :], gate_b).then_inc(s_ew, 16)

            def pair_loads(c, first, last):
                i = c.i
                if not last:
                    c.pair(s_xn, 0)
                    sp.dma_start(xa[:, :], x_tb[bass.ds(i * 128 + 128, 128), :]).then_inc(s_xa, 16)
                if not first:
                    c.pair(s_y, -1)
                    sp.dma_start(xb[:, :], x_tb[bass.ds(i * 128, 128), :]).then_inc(s_xb, 16)

            run_pairs(sp, pair_loads)

            def load_x(tile, n):
                sp.dma_start(xo[:, n, :, :], x_tbd[:, bass.ds(tile * FG, FG), :]).then_inc(s_xo[n], 16)

            def store_and_reload(c, first, last):
                for n in range(2):
                    c.at_least(s_fr, 2, n + 1)
                    sp.dma_start(out[:, bass.ds(c.i * (2 * FG) + n * FG, FG), :], res[:, n, :, :])\
                        .then_inc(s_out[n], 16)
                    c.at_least(s_out[n], 16, 16)
                    if not last:
                        load_x(c.i * 2 + (n + 2), n)

            for n in range(2):
                load_x(n, n)
            run_tiles(sp, store_and_reload)
        @block.gpsimd
        def _(pool):
            pool.memset(kst[:, :, Q * S:], 0.0).then_inc(s_kc, 1)
            pool.memset(mhalf[:, :], -0.5).then_inc(s_pm, 1)
            pool.memset(zsum[:, :], 0.0).then_inc(s_zs, 1)

            def rstd(wait, mv, ve, rs, s_ve, s_rs, wait_ve, hold=lambda: None):
                wait()
                hold()
                pool.tensor_scalar(ve[:, :], mv[:, 1:2], EPS, None, ALU.add).then_inc(s_ve, 1)
                wait_ve()
                pool.tensor_tensor(rs[:, :], ve[:, :], mhalf[:, :], ALU.pow).then_inc(s_rs, 1)

            pool.wait_ge(s_pm, 1)
            rstd(lambda: pool.wait_ge(s_x2, 1), mv1, ve1, rs1, s_xv, s_xs, lambda: pool.wait_ge(s_xv, 1))
            def split_weights(n):
                step, group = divmod(n, 4)
                blocks = slice(4 * group, min(4 * group + 4, 13))
                if step == 0:
                    pool.wait_ge(s_ws, len(WEIGHT_FACTORS))
                    pool.tensor_copy(w3[:, 0, blocks, :], wf[:, blocks, :]).then_inc(s_wh, 1)
                elif step == 1:
                    pool.wait_ge(s_wh, group + 1)
                    pool.tensor_tensor(wf[:, blocks, :], wf[:, blocks, :], w3[:, 0, blocks, :], ALU.subtract)\
                        .then_inc(s_wr, 1)
                    pool.wait_ge(s_wr, group + 1)
                    pool.tensor_copy(w3[:, 1, blocks, :], wf[:, blocks, :]).then_inc(s_wm, 1)
                elif step == 2:
                    pool.wait_ge(s_wm, group + 1)
                    pool.tensor_tensor(w3[:, 2, blocks, :], wf[:, blocks, :], w3[:, 1, blocks, :], ALU.subtract)\
                        .then_inc(s_wl, 1)

            for k in range(KSTEPS):
                if k >= 2:
                    split_weights(k - 2)
                pool.wait_ge(s_kvm, k + 1)
                part = kst[:, k * KG:(k + 1) * KG, :]
                pool.tensor_tensor(part[:, :, 2 * S:3 * S], kr[:, k % 2, :, :], part[:, :, S:2 * S],
                                   ALU.subtract).then_inc(s_kl, 1)

            def finish(c, k):
                rstd(lambda: c.pair(s_y2, k), mv2, ve2, rs2, s_yv, s_ys, lambda: c.pair(s_yv, k),
                     c.hold)
                c.pair(s_z, k)
                c.pair(s_zs, k)
                pool.tensor_tensor(zsum[:, :], zsum[:, :], z[:, :], ALU.add).then_inc(s_zs, 1)

            def pair_work(c, first, last):
                if not last:
                    rstd(lambda: c.pair(s_x2, 1), mv1, ve1, rs1, s_xv, s_xs, lambda: c.pair(s_xv, 1),
                         c.hold)
                if not first:
                    finish(c, -1)

            run_pairs(pool, pair_work)
            c = Counts(pool, PAIRS - 1)
            finish(c, 0)

            pool.wait_ge(s_gv, 5)

            def add_expert(c, n, e):
                k = n * E + e
                row = c.i * (2 * FG) + (n * FG + FV)
                if e == 0:
                    c.at_least(s_fc, 2, n + 1)
                c.at_least(s_fh, 2 * E, k + 1)
                c.at_least(s_fx, 2 * E, k - 2 + 1)
                pool.tensor_tensor(gated[:, e % 2, :], gl[:, k % 4, :],
                                   tile_gates[:, n, FV, e:e + 1].to_broadcast([128, T]), ALU.mult)\
                    .then_inc(s_fm, 1)
                if e == 0:
                    c.at_least(s_fT, 2, n - 1)
                c.at_least(s_fm, 2 * E, k + 1)
                c.at_least(s_fx, 2 * E, k)
                before = attn_all[:, :, bass.ds(row, 1)].rearrange("p t b -> p (t b)") if e == 0 \
                    else acc[:, n, FV, :]
                pool.tensor_tensor(acc[:, n, FV, :], gated[:, e % 2, :], before, ALU.add).then_inc(s_fx, 1)

            def tiles(c, first, last):
                for n in range(2):
                    for e in range(E):
                        add_expert(c, n, e)

            run_tiles(pool, tiles)

        @block.scalar
        def _(act):
            act.dma_start(xa[:, :], x_tb[0:128, :]).then_inc(s_xa, 16)
            act.dma_start(bi[:, :, :], b_ih).then_inc(s_bw, 16)
            act.dma_start(bh[:, :, :], b_hh).then_inc(s_bw, 16)
            act.dma_start(bo[:, :], b_out).then_inc(s_bw, 16)
            act.dma_start(wf[:, :, :], w_gates).then_inc(s_w, 16)
            act.wait_ge(s_xT, 1)

            def x_hi(u):
                cols = slice(u * B, (u + 1) * B)
                act.copy(xq[:, 0, cols], ps_xT[:, cols]).then_inc(s_xh, 1)

            x_hi(0)
            act.wait_ge(s_xl, 1)
            x_hi(1)

            for k in range(KSTEPS + 1):
                if k < KSTEPS:
                    p, rows = k % 2, slice(k * KG, (k + 1) * KG)
                    act.wait_ge(s_kvp, 3 * k + 1)
                    act.activation(kst[:, rows, 0:S], bank[p][:, 0:KG * S].rearrange("p (b s) -> p b s", b=KG),
                                   ACT.Copy, scale=0.5).then_inc(s_kvh, 1)
                    act.wait_ge(s_kvp, 3 * k + 2)
                    if k >= 2:
                        act.wait_ge(s_kvr, 3 * (k - 1))
                    act.copy(v0hi[:, p, :, :], bank[2 + p][:, :].rearrange("p (b j) -> p b j", b=KG))\
                        .then_inc(s_kvh, 1)
                    act.wait_ge(s_kvp, 3 * k + 3)
                    act.copy(v1hi[:, p, :, :], bank[4 + p][:, :].rearrange("p (b j) -> p b j", b=KG))\
                        .then_inc(s_kvh, 1)
                if k >= 1:
                    p, rows = (k - 1) % 2, slice((k - 1) * KG, k * KG)
                    act.wait_ge(s_kvr, 3 * k)
                    if k >= 3:
                        act.wait_ge(s_vl, k - 2)
                    act.copy(kst[:, rows, S:2 * S], kr[:, p, :, :])
                    act.copy(v1mid[:, p, :, :], v1r[:, p, :, :]).then_inc(s_kvm, 1)
            def gates_tanh(c, k, g):
                c.turn(s_gates, k)
                act.activation(tg[g][:, :, :], ps_gates[g], ACT.Tanh).then_inc(s_tg, 1)

            def c_tanh(c, k, g):
                c.turn(s_c, k)
                act.activation(tc[g][:, :], c2[g][:, :], ACT.Tanh, scale=0.5).then_inc(s_tc, 1)

            def exps(c, k, g):
                c.turn(s_mx, k)
                act.activation(expo[g][:, :], ps_row[g], ACT.Exp, bias=neg_max[g][:, 0:1],
                               accum_out=ps_den[g]).then_inc(s_ex, 1)

            def attn(c, k, g, u):
                c.turn(s_vs, k)
                act.activation(atq[g][:, 0, :], at_in[g][:, :], ACT.Tanh, bias=bo[:, 0:1])
                c.pair(s_yT, -1)
                act.activation(attn_out(u, g), at_in[g][:, :], ACT.Tanh, bias=bo[:, 0:1])\
                    .then_inc(s_at, 1)

            def save_attn(c, k):
                c.turn(s_at, TURNS * (k + 1) - 1)
                i = c.i
                act.copy(attn_all[:, bass.ds((i + k) * U, U), :].rearrange("p u b -> p (u b)"), at[:, :])

            def store_z(c, k):
                c.pair(s_zT, k)
                i = c.i
                dst = zT[:, :, bass.ds((i + k) * U, U)].rearrange("p b u -> p u b")
                act.copy(dst, ps_zT.rearrange("p (u b) -> p u b", u=U)).then_inc(s_zc, 1)

            def up_to_last_attn(c, u, first, last):
                k0, k1 = u * G, u * G + 1
                gates_tanh(c, k0, 0)
                c_tanh(c, k0, 0)
                if u == 0 and not first:
                    save_attn(c, -1)
                gates_tanh(c, k1, 1)
                c_tanh(c, k1, 1)
                exps(c, k0, 0)
                exps(c, k1, 1)
                attn(c, k0, 0, u)
                if not last:
                    c.step(s_xg, u)
                    c.pair(s_xT, 1)
                    c.step(s_xl, U - 1 + u)
                    x_hi(u)
                if u == 1 and not first:
                    store_z(c, -1)

            def head(c, first, last):
                up_to_last_attn(c, 0, first, last)
                attn(c, 1, 1, 0)
                up_to_last_attn(c, 1, first, last)

            def tail(c, last):
                attn(c, TURNS - 1, 1, U - 1)

            run_pairs_in_two(act, head, tail)
            save_attn(Counts(act, PAIRS - 1), 0)
            store_z(Counts(act, PAIRS - 1), 0)

            act.wait_ge(s_gv, 3)
            act.activation(ge[:, :], lg[:, :], ACT.Exp, bias=ntop[:, 0:1]).then_inc(s_ga, 1)

            def tiles(c, first, last):
                for n in range(2 * E):
                    c.at_least(s_fp, 2 * E, n + 1)
                    for_vector, for_pool = bank[n % 4][:, 0:FV * T], bank[n % 4][:, FV * T:]
                    c.at_least(s_fm, 2 * E, n - 4 + 1)
                    act.activation(gl[:, n % 4, :], for_pool, ACT.Gelu, bias=eb[:, n % E:n % E + 1])\
                        .then_inc(s_fh, 1)
                    act.activation(for_vector, for_vector, ACT.Gelu, bias=eb[:, n % E:n % E + 1]).then_inc(s_fg, 1)

            run_tiles(act, tiles)

        @block.vector
        def _(dve):
            dve.memset(ones[:, :], 1.0).then_inc(s_ms, 1)
            dve.memset(onesf[:, :], 1.0)
            for g in range(G):
                dve.memset(c2[g][:, :], 0.0)
                dve.memset(hq[g][:, :, :], 0.0)
                dve.memset(atq[g][:, :, :], 0.0)
                if g < G - 1:
                    dve.memset(alpha[g][:, :], 0.0)
            dve.memset(alpha[G - 1][:, :], 0.0).then_inc(s_ms, 1)

            def ln1_apply(wait_rstd, wait_xn_read):
                wait_rstd()
                wait_xn_read()
                dve.tensor_scalar(xn[:, :], xa[:, :], mv1[:, 0:1], rs1[:, 0:1], ALU.subtract, ALU.mult)\
                    .then_inc(s_xn, 1)

            def x_mid(c, k, u):
                cols = slice(u * B, (u + 1) * B)
                c.step(s_xh, k)
                dve.tensor_tensor(xr[:, cols], ps_xT[:, cols], xq[:, 0, cols], ALU.subtract)
                dve.tensor_tensor(xq[:, 1, cols], ps_xT[:, cols], xq[:, 0, cols], ALU.subtract).then_inc(s_xm, 1)

            def x_lo(c, k, u):
                cols = slice(u * B, (u + 1) * B)
                c.step(s_xm, k)
                dve.tensor_tensor(xq[:, 2, cols], xr[:, cols], xq[:, 1, cols], ALU.subtract).then_inc(s_xl, 1)

            dve.wait_ge(s_xa, 16)
            dve.bn_stats(st1[:, :], xa[:, :]).then_inc(s_x1, 1)
            dve.wait_ge(s_x1, 1)
            dve.bn_aggr(mv1[:, :], st1[:, :]).then_inc(s_x2, 1)

            ln1_apply(lambda: dve.wait_ge(s_xs, 1), lambda: None)
            for u in range(U):
                x_mid(Counts(dve, 0), u, u)
                x_lo(Counts(dve, 0), u, u)


            def biases_and_weights(n):
                if n == 0:
                    dve.wait_ge(s_bw, 48)
                    dve.tensor_tensor(bi[:, :, :], bi[:, :, :], bh[:, :, :], ALU.add).then_inc(s_b, 1)
                elif n == 1:
                    dve.wait_ge(s_w, 16)
                    for first, count, factor in WEIGHT_FACTORS:
                        w = wf[:, first:first + count, :]
                        dve.tensor_scalar(w, w, factor, None, ALU.mult).then_inc(s_ws, 1)
                elif n == 2:
                    dve.wait_ge(s_b, 1)
                    for m in (0, 1, 3):
                        dve.tensor_scalar(bi[:, m, :], bi[:, m, :], 0.5, None, ALU.mult).then_inc(s_b, 1)
                elif n == 3:
                    dve.wait_ge(s_b, 4)
                    dve.tensor_copy(bhi[:, :, :], bi[:, :, :]).then_inc(s_b, 1)
                elif n == 4:
                    dve.wait_ge(s_b, 5)
                    dve.scalar_tensor_tensor(out=bh[:, :, :], in0=bhi[:, :, :], scalar=mask(3), in1=bi[:, :, :],
                                             op0=ALU.mult, op1=ALU.add).then_inc(s_b, 1)
                elif n == 5:
                    dve.wait_ge(s_b, 6)
                    dve.tensor_copy(bhi[:, :, :], bh[:, :, :]).then_inc(s_b, 1)
                elif n == 6:
                    dve.wait_ge(s_b, 7)
                    dve.scalar_tensor_tensor(out=b3[:, :, :], in0=bhi[:, :, :], scalar=mask(4), in1=bh[:, :, :],
                                             op0=ALU.mult, op1=ALU.add).then_inc(s_wl, 1)

            for k in range(KSTEPS + 1):
                if k < KSTEPS:
                    p, rows = k % 2, slice(k * KG, (k + 1) * KG)
                    dve.wait_ge(s_kvh, 3 * k + 1)
                    if k >= 2:
                        dve.wait_ge(s_kl, k - 1)
                    dve.scalar_tensor_tensor(
                        out=kr[:, p, :, :], in0=bank[p][:, 0:KG * S].rearrange("p (b s) -> p b s", b=KG),
                        scalar=0.5, in1=kst[:, rows, 0:S], op0=ALU.mult, op1=ALU.subtract).then_inc(s_kvr, 1)
                    dve.wait_ge(s_kvh, 3 * k + 2)
                    dve.scalar_tensor_tensor(
                        out=vst[:, rows, 0, :], in0=v0hi[:, p, :, :], scalar=mask(0),
                        in1=bank[2 + p][:, :].rearrange("p (b j) -> p b j", b=KG),
                        op0=ALU.mult, op1=ALU.add).then_inc(s_kvr, 1)
                    dve.wait_ge(s_kvh, 3 * k + 3)
                    if k >= 2:
                        dve.wait_ge(s_vl, k - 1)
                    dve.scalar_tensor_tensor(
                        out=v1r[:, p, :, :], in0=v1hi[:, p, :, :], scalar=mask(1),
                        in1=bank[4 + p][:, :].rearrange("p (b j) -> p b j", b=KG),
                        op0=ALU.mult, op1=ALU.add).then_inc(s_kvr, 1)
                if k < KSTEPS:
                    biases_and_weights(k)
                if k >= 1:
                    p, rows = (k - 1) % 2, slice((k - 1) * KG, k * KG)
                    dve.wait_ge(s_kvm, k)
                    dve.scalar_tensor_tensor(
                        out=vst[:, rows, 1, :], in0=v1mid[:, p, :, :], scalar=mask(2), in1=v1r[:, p, :, :],
                        op0=ALU.mult, op1=ALU.add).then_inc(s_vl, 1)
            def c_terms(c, k, g):
                t_in, t_forget, t_cell = (tg[g][:, m, :] for m in range(3))
                c.turn(s_tg, k)
                dve.scalar_tensor_tensor(out=in_term[g][:, :], in0=t_in, scalar=1.0, in1=t_cell,
                                         op0=ALU.add, op1=ALU.mult)
                dve.scalar_tensor_tensor(out=forget_term[g][:, :], in0=t_forget, scalar=1.0, in1=c2[g][:, :],
                                         op0=ALU.add, op1=ALU.mult).then_inc(s_ct, 1)

            def c_sum(c, k, g):
                c.turn(s_ct, k)
                dve.scalar_tensor_tensor(out=c2[g][:, :], in0=forget_term[g][:, :], scalar=0.5,
                                         in1=in_term[g][:, :], op0=ALU.mult, op1=ALU.add).then_inc(s_c, 1)

            def h_hi(c, k, g):
                t_out = tg[g][:, 3, :]
                c.turn(s_tc, k)
                dve.scalar_tensor_tensor(out=hq[g][:, 0, :], in0=t_out, scalar=1.0, in1=tc[g][:, :],
                                         op0=ALU.add, op1=ALU.mult)
                dve.scalar_tensor_tensor(out=h2[g][:, :], in0=t_out, scalar=1.0, in1=tc[g][:, :],
                                         op0=ALU.add, op1=ALU.mult).then_inc(s_h, 1)

            def h_mid(c, k, g):
                c.turn(s_h, k)
                dve.tensor_tensor(hr[g][:, :], h2[g][:, :], hq[g][:, 0, :], ALU.subtract)
                dve.tensor_tensor(hq[g][:, 1, :], h2[g][:, :], hq[g][:, 0, :], ALU.subtract).then_inc(s_hm, 1)

            def h_lo(c, k, g):
                c.turn(s_hm, k)
                dve.tensor_tensor(hq[g][:, 2, :], hr[g][:, :], hq[g][:, 1, :], ALU.subtract).then_inc(s_hl, 1)

            def score_sum(c, k, g):
                c.turn(s_sp, k)
                dve.tensor_reduce(sc[g][:, :, :], ps_sc[g], AX_X, ALU.add).then_inc(s_ss, 1)

            def row_max(c, k, g):
                c.turn(s_row, k)
                dve.tensor_reduce(neg_max[g][:, :], ps_row[g], AX_X, ALU.max, negate=True).then_inc(s_mx, 1)

            def one_over_sum(c, k, g):
                c.turn(s_ex, k)
                dve.reciprocal(rden[g][:, :], ps_den[g]).then_inc(s_rd, 1)

            def normalise(c, k, g):
                c.turn(s_rd, k)
                for first, count in ((0, SA), (SA, SB)):
                    last = dve.tensor_scalar(
                        alpha[g][:, Q * first:Q * (first + count)].rearrange("p (k s) -> p k s", k=Q),
                        expo[g][:, first:first + count].unsqueeze(1).to_broadcast([NB, Q, count]),
                        rden[g][:, 0:1], None, ALU.mult)
                last.then_inc(s_al, 1)

            def alpha_hi(c, k, g):
                c.turn(s_aT, k)
                dve.tensor_copy(aq[g][:, 0, :, :], ps_alT[g]).then_inc(s_ah, 1)

            def alpha_mid(c, k, g):
                c.turn(s_ah, k)
                dve.tensor_tensor(ar[g][:, :, :], ps_alT[g], aq[g][:, 0, :, :], ALU.subtract)
                dve.tensor_tensor(aq[g][:, 1, :, :], ps_alT[g], aq[g][:, 0, :, :], ALU.subtract)\
                    .then_inc(s_am, 1)

            def alpha_lo(c, k, g):
                c.turn(s_am, k)
                dve.tensor_tensor(aq[g][:, 2, :, :], ar[g][:, :, :], aq[g][:, 1, :, :], ALU.subtract)\
                    .then_inc(s_as, 1)

            def value_sum(c, k, g):
                c.turn(s_vp, k)
                dve.tensor_reduce(at_in[g][:, :], ps_val[g], AX_X, ALU.add).then_inc(s_vs, 1)

            def attn_mid(c, k, g, u):
                c.turn(s_at, k)
                dve.tensor_tensor(at_r[g][:, :], attn_out(u, g), atq[g][:, 0, :], ALU.subtract)
                dve.tensor_tensor(atq[g][:, 1, :], attn_out(u, g), atq[g][:, 0, :], ALU.subtract)\
                    .then_inc(s_tm, 1)

            def attn_lo(c, k, g):
                c.turn(s_tm, k)
                dve.tensor_tensor(atq[g][:, 2, :], at_r[g][:, :], atq[g][:, 1, :], ALU.subtract)\
                    .then_inc(s_ts, 1)

            def ln2_add(c, k):
                c.pair(s_yT, k)
                c.pair(s_xb, k, 16)
                dve.tensor_tensor(y[:, :], ps_y, xb[:, :], ALU.add).then_inc(s_y, 1)

            def ln2_stats(c, k):
                c.pair(s_y, k)
                dve.bn_stats(st2[:, :], y[:, :]).then_inc(s_y1, 1)

            def ln2_mean_var(c, k):
                c.pair(s_y1, k)
                c.hold()
                dve.bn_aggr(mv2[:, :], st2[:, :]).then_inc(s_y2, 1)

            def ln2_apply(c, k):
                c.pair(s_ys, k)
                dve.tensor_scalar(z[:, :], y[:, :], mv2[:, 0:1], rs2[:, 0:1], ALU.subtract, ALU.mult)\
                    .then_inc(s_z, 1)

            def to_value_sum(c, u, first, last):
                k0, k1 = u * G, u * G + 1
                ln1, ln2 = (u == 0 and not last), (u == 1 and not first)
                c_terms(c, k0, 0)
                c_sum(c, k0, 0)
                h_hi(c, k0, 0)
                h_mid(c, k0, 0)
                h_lo(c, k0, 0)
                c_terms(c, k1, 1)
                c_sum(c, k1, 1)
                if ln1:
                    c.pair(s_xa, 1, 16)
                    dve.bn_stats(st1[:, :], xa[:, :]).then_inc(s_x1, 1)
                h_hi(c, k1, 1)
                h_mid(c, k1, 1)
                h_lo(c, k1, 1)
                score_sum(c, k0, 0)
                if ln2:
                    ln2_add(c, -1)
                    ln2_stats(c, -1)
                if ln1:
                    c.pair(s_x1, 1)
                    c.hold()
                    dve.bn_aggr(mv1[:, :], st1[:, :]).then_inc(s_x2, 1)
                row_max(c, k0, 0)
                one_over_sum(c, k0, 0)
                normalise(c, k0, 0)
                if ln1:
                    ln1_apply(lambda: c.pair(s_xs, 1), lambda: c.pair(s_xT, 0))
                if ln2:
                    ln2_mean_var(c, -1)
                score_sum(c, k1, 1)
                alpha_hi(c, k0, 0)
                alpha_mid(c, k0, 0)
                alpha_lo(c, k0, 0)
                row_max(c, k1, 1)
                one_over_sum(c, k1, 1)
                normalise(c, k1, 1)
                if ln2:
                    ln2_apply(c, -1)
                alpha_hi(c, k1, 1)
                alpha_mid(c, k1, 1)
                alpha_lo(c, k1, 1)
                value_sum(c, k0, 0)

            def from_attention(c, u, last):
                k0, k1 = u * G, u * G + 1
                attn_mid(c, k0, 0, u)
                if not last:
                    x_mid(c, U + u, u)
                attn_lo(c, k0, 0)
                if not last:
                    x_lo(c, U + u, u)
                value_sum(c, k1, 1)
                attn_mid(c, k1, 1, u)
                attn_lo(c, k1, 1)

            def head(c, first, last):
                to_value_sum(c, 0, first, last)
                from_attention(c, 0, last)
                to_value_sum(c, 1, first, last)

            def tail(c, last):
                from_attention(c, 1, last)

            run_pairs_in_two(dve, head, tail)
            c = Counts(dve, PAIRS - 1)
            ln2_add(c, 0)
            ln2_stats(c, 0)
            ln2_mean_var(c, 0)
            ln2_apply(c, 0)

            dve.wait_ge(s_gt, 1)
            dve.tensor_copy(pooled[:, :], bank[4][:, 0:B]).then_inc(s_gv, 1)
            dve.wait_ge(s_gt, 2)
            dve.wait_ge(s_ew, 64)
            dve.tensor_tensor(lg[:, :], bank[4][0:B, B:B + E], gb[:, :], ALU.add).then_inc(s_gv, 1)
            dve.wait_ge(s_gv, 2)
            dve.max(top[:, :], lg[:, :]).then_inc(s_b, 1)
            dve.wait_ge(s_b, 8)
            dve.tensor_scalar(ntop[:, :], top[:, 0:1], -1.0, None, ALU.mult).then_inc(s_gv, 1)
            dve.tensor_scalar(keep[:, :], lg[:, :], top[:, 1:2], None, ALU.is_ge).then_inc(s_b, 1)
            dve.wait_ge(s_ga, 1)
            dve.wait_ge(s_b, 9)
            dve.tensor_tensor(gk[:, :], ge[:, :], keep[:, :], ALU.mult).then_inc(s_b, 1)
            dve.wait_ge(s_b, 10)
            dve.tensor_reduce(gs[:, :], gk[:, :], AX_X, ALU.add).then_inc(s_b, 1)
            dve.wait_ge(s_b, 11)
            dve.reciprocal(gr[:, :], gs[:, :]).then_inc(s_b, 1)
            dve.wait_ge(s_b, 12)
            dve.tensor_scalar(ge[:, :], gk[:, :], gr[:, 0:1], None, ALU.mult).then_inc(s_b, 1)
            dve.wait_ge(s_b, 13)
            dve.tensor_tensor(gd[:, :, :], ge[:, :].unsqueeze(1).to_broadcast([B, B, E]),
                              cst[0:B, C_ID:C_ID + B].unsqueeze(2).to_broadcast([B, B, E]), ALU.mult)\
                .then_inc(s_gv, 1)
            dve.wait_ge(s_gt, 3)
            dve.tensor_copy(gates[:, :, :], bank[5][:, :].rearrange("p (b e) -> p b e", e=E)).then_inc(s_gv, 1)
            dve.wait_ge(s_gv, 5)

            def add_expert(c, n, e):
                k = n * E + e
                c.at_least(s_fg, 2 * E, k + 1)
                if e == 0:
                    c.at_least(s_fT, 2, n - 1)
                    c.at_least(s_fc, 2, n + 1)
                for q in range(FV):
                    if q != 1:
                        c.at_least(s_fv, 2 * E * FV, (k - 1) * FV + (2 if q == 0 else q + 1))
                    row = c.i * (2 * FG) + (n * FG + q)
                    before = attn_all[:, :, bass.ds(row, 1)].rearrange("p t b -> p b t") if e == 0 \
                        else acc[:, n, q:q + 1, :]
                    dve.scalar_tensor_tensor(
                        out=acc[:, n, q:q + 1, :], in0=bank[k % 4][:, q * T:(q + 1) * T].unsqueeze(1),
                        scalar=tile_gates[:, n, q, e:e + 1], in1=before, op0=ALU.mult, op1=ALU.add)\
                        .then_inc(s_fv, 1)

            def copy_gates(c, n):
                p = n % 2
                dve.tensor_copy(tile_gates[:, p, :, :], gates[:, bass.ds(c.i * (2 * FG) + n * FG, FG), :])\
                    .then_inc(s_fc, 1)

            def result(c, n, ago):
                p, back = (n - ago) % 2, (1 if ago > n else 0)
                c.at_least(s_fT, 2, n - ago + 1)
                c.at_least(s_xo[p], 16, 16 * (1 - back))
                dve.tensor_tensor(res[:, p, :, :], bank[6 + p][:, :].rearrange("p (b d) -> p b d", b=FG),
                                  xo[:, p, :, :], ALU.add).then_inc(s_fr, 1)

            def tiles(c, first, last):
                for n in range(2):
                    for e in range(E):
                        add_expert(c, n, e)
                        if e == 6 and not (first and n == 0):
                            result(c, n, 1)
                        if e == 6 and not (last and n == 1):
                            copy_gates(c, n + 1)
                if last:
                    result(c, 1, 0)

            copy_gates(Counts(dve, 0), 0)
            run_tiles(dve, tiles)

        @block.tensor
        def _(pe):
            mm = pe.matmul
            pe.wait_ge(s_kw, 16 * 3)
            pe.wait_ge(s_xn, 1)
            pe.transpose(ps_xT, xn[:, :], ident).then_inc(s_xT, 1)
            for k in range(KSTEPS):
                p = k % 2
                if k % (KSTEPS // 4) == 0:
                    pe.wait_ge(s_ctx[k // (KSTEPS // 4)], 16)
                def reusable(product):
                    if k >= 2:
                        pe.wait_ge(s_kvr, 3 * (k - 2) + product + 1)

                reusable(0)
                mm(bank[p][:, 0:KG * S], wq[:, :], ctxT[:, k * KG:(k + 1) * KG, 0:S], start=True, stop=True)\
                    .then_inc(s_kvp, 1)
                reusable(1)
                for q in range(KG):
                    for half in range(2):
                        last = mm(bank[2 + p][half * SA:(half + 1) * SA, q * 128:(q + 1) * 128],
                                  ctxT[:, k * KG + q, 0:SA], wo[:, :], start=True, stop=True)
                last.then_inc(s_kvp, 1)
                reusable(2)
                for q in range(KG):
                    last = mm(bank[4 + p][:, q * 128:(q + 1) * 128], ctxT[:, k * KG + q, :], wo[:, :],
                              start=True, stop=True)
                last.then_inc(s_kvp, 1)
            pe.wait_ge(s_kvr, 3 * KSTEPS)

            def h_gates(g, products):
                for m in range(4):
                    for wp, hp in products:
                        mm(ps_gates[g][:, m, :], w3[:, wp, 8 + m, :], hq[g][:, hp, :],
                           start=(m == 0 and (wp, hp) == PRODUCTS[0]), stop=False, skip_group_check=True)

            def x_gates(g, u, gates_=range(4)):
                for m in gates_:
                    o = ps_gates[g][:, m, :]
                    mm(o, b3[:, m, :], ones[:, 0:NB], start=False, stop=False, skip_group_check=True)
                    for wp, xp in PRODUCTS:
                        cols = slice(u * B + g * NB, u * B + (g + 1) * NB)
                        last = mm(o, w3[:, wp, m, :], xq[:, xp, cols], start=False, stop=False,
                                  skip_group_check=True)
                if g == G - 1:
                    last.then_inc(s_xg, 1)

            def attn_gates(c, k, g):
                c.turn(s_ts, k - G)
                o = ps_gates[g]
                for m in range(4):
                    for wp, ap in PRODUCTS:
                        last = mm(o[:, m, :], w3[:, wp, 4 + m, :], atq[g][:, ap, :], start=False,
                                  stop=(wp, ap) == PRODUCTS[-1], skip_group_check=True)
                last.then_inc(s_gates, 1)

            def scores(c, k, g):
                c.turn(s_hl, k)
                for j in range(NB):
                    for pack in range(2):
                        last = mm(ps_sc[g][:, pack, j, :], kst[:, g * NB + j, pack * 128:(pack + 1) * 128],
                                  hq[g][:, :, j], start=True, stop=True)
                last.then_inc(s_sp, 1)

            def h_out(g, opens, products=range(len(PRODUCTS))):
                for n in products:
                    wp, hp = PRODUCTS[n]
                    mm(ps_val[g][:, :, 0], w3[:, wp, 12, :], hq[g][:, hp, :], start=(opens and n == 0),
                       stop=False, skip_group_check=True)

            def rows(c, k, g):
                c.turn(s_ss, k)
                for pack in range(2):
                    last = mm(ps_row[g], sc[g][:, pack, :], sel(pack), start=(pack == 0), stop=(pack == 1))
                last.then_inc(s_row, 1)

            def turn_alpha(c, k, g, before):
                c.turn(s_al, k)
                before()
                id_nb = cst[0:NB, C_ID:C_ID + NB]
                for pack in range(2):
                    last = pe.transpose(ps_alT[g][:, pack, :], alpha[g][:, pack * 128:(pack + 1) * 128], id_nb)
                last.then_inc(s_aT, 1)

            def values(c, k, g, rows_):
                c.turn(s_as, k)
                for j in rows_:
                    for pack in range(2):
                        last = mm(ps_val[g][:, j, :], vst[:, g * NB + j, pack, :], aq[g][:, :, pack, j],
                                  start=False, stop=(pack == 1), skip_group_check=True)
                if rows_[-1] == NB - 1:
                    last.then_inc(s_vp, 1)

            pe.wait_ge(s_wl, 5)
            pe.wait_ge(s_xl, U)
            pe.wait_ge(s_ms, 2)
            h_gates(0, PRODUCTS)
            x_gates(0, 0)
            pe.wait_ge(s_kc, 1)
            pe.wait_ge(s_kl, KSTEPS)
            pe.wait_ge(s_vl, KSTEPS)
            cut = 24

            def pair_work(c, first, last):
                for u in range(U):
                    last_step = last and u == U - 1
                    k0, k1 = u * G, u * G + 1
                    attn_gates(c, k0, 0)
                    c.turn(s_vs, k1 - G)
                    h_gates(1, PRODUCTS)
                    x_gates(1, u)
                    attn_gates(c, k1, 1)
                    if u == 0 and not first:
                        pe.transpose(ps_y, at[:, :], ident).then_inc(s_yT, 1)
                    if not last_step:
                        c.turn(s_h, k0)
                        h_gates(0, WITH_HI)
                        c.turn(s_hm, k0)
                        h_gates(0, WITH_MID)
                    scores(c, k0, 0)
                    if not last_step:
                        h_gates(0, WITH_LO)
                    h_out(0, last_step)
                    rows(c, k0, 0)
                    scores(c, k1, 1)
                    turn_alpha(c, k0, 0, lambda: h_out(1, False, range(0, 1)))
                    h_out(1, False, range(1, len(PRODUCTS)))
                    rows(c, k1, 1)
                    if not last_step:
                        c.step(s_xl, u + 1)
                        x_gates(0, 1 - u, (0, 1))
                    values(c, k0, 0, range(cut))
                    turn_alpha(c, k1, 1, lambda: values(c, k0, 0, range(cut, cut + 1)))
                    if not last_step:
                        x_gates(0, 1 - u, (2,))
                    if u == 0 and not last:
                        c.pair(s_xn, 1)
                        c.step(s_xl, U - 1)
                        pe.transpose(ps_xT, xn[:, :], ident).then_inc(s_xT, 1)
                    if u == 1 and not first:
                        c.pair(s_z, -1)
                        pe.transpose(ps_zT, z[:, :], ident).then_inc(s_zT, 1)
                    if not last_step:
                        x_gates(0, 1 - u, (3,))
                    values(c, k0, 0, range(cut + 1, NB))
                    values(c, k1, 1, range(NB))

            run_pairs(pe, pair_work)
            c = Counts(pe, PAIRS - 1)
            for g in range(G):
                c.turn(s_at, TURNS - G + g)
            c.pair(s_y, -1)
            pe.transpose(ps_y, at[:, :], ident).then_inc(s_yT, 1)
            c.pair(s_z, 0)
            c.pair(s_zc, -1)
            pe.transpose(ps_zT, z[:, :], ident).then_inc(s_zT, 1)

            pe.wait_ge(s_zs, PAIRS + 1)
            pe.wait_ge(s_ew, 64)
            mm(bank[4][:, 0:B], zsum[:, :], fold, start=True, stop=True).then_inc(s_gt, 1)
            pe.wait_ge(s_gv, 1)
            mm(bank[4][0:B, B:B + E], pooled[:, :], gw[:, :], start=True, stop=True).then_inc(s_gt, 1)
            pe.wait_ge(s_gv, 4)
            mm(bank[5][:, :], onesf[:, :], gd[:, :, :].rearrange("p b e -> p (b e)"), start=True, stop=True)\
                .then_inc(s_gt, 1)
            pe.wait_ge(s_zc, PAIRS)

            def tile_back(c, n, ago):
                p = (n - ago) % 2
                c.at_least(s_fv, 2 * E * FV, (n - ago + 1) * E * FV)
                c.at_least(s_fx, 2 * E, (n - ago + 1) * E)
                for q in range(FG):
                    last = pe.transpose(bank[6 + p][:, q * 128:(q + 1) * 128], acc[:, p, q, :], ident)
                last.then_inc(s_fT, 1)

            def tiles(c, first, last):
                for n in range(2):
                    for e in range(E):
                        k = n * E + e
                        c.at_least(s_fv, 2 * E * FV, (k - 4 + 1) * FV)
                        pe.matmul(bank[k % 4][:, :], ew[:, e, :],
                                  zT[:, bass.ds(c.i * (2 * FG) + n * FG, FG), :].rearrange("p b t -> p (b t)"),
                                  start=True, stop=True).then_inc(s_fp, 1)
                        if e == 6 and not (first and n == 0):
                            tile_back(c, n, 1)
                if last:
                    tile_back(c, 1, 0)

            run_tiles(pe, tiles)


def kernel(x, ctx_1024, L0_xattn_W_ih, L0_xattn_W_hh, L0_xattn_b_ih, L0_xattn_b_hh, L0_xattn_Wq,
           L0_xattn_Wout, L0_xattn_b_out, L0_ffn_gate_w, L0_ffn_gate_b, L0_ffn_expert_w, L0_ffn_expert_b):
    import concourse.bacc as bacc
    from concourse.bass_utils import run_bass_kernel_spmd as run

    x, context = np.asarray(x), np.asarray(ctx_1024)
    w_ih, w_hh, w_out = (np.asarray(a) for a in (L0_xattn_W_ih, L0_xattn_W_hh, L0_xattn_Wout))
    c_t = context.transpose(2, 0, 1)
    ctx_dup = np.zeros((D, B, 128), np.float32)
    ctx_dup[:, :, :S] = c_t
    for k in (1, 2):
        ctx_dup[:, :, SA + k * SB:SA + (k + 1) * SB] = c_t[:, :, SA:]
    w_gates = np.concatenate([w_ih[:, :D].T, w_ih[:, D:].T, w_hh.T, w_out[:, D:].T], axis=1)

    def bias_rows(b):
        rows = np.zeros((128, 4 * 128), np.float32)
        rows[[0, 32, 64]] = np.asarray(b)
        return rows.reshape(128, 4, 128)

    arrays = {
        "x_tbd": x.transpose(1, 0, 2),
        "ctx_dup": ctx_dup,
        "w_gates": w_gates.reshape(128, 13, 128),
        "b_ih": bias_rows(L0_xattn_b_ih),
        "b_hh": bias_rows(L0_xattn_b_hh),
        "w_q": np.asarray(L0_xattn_Wq),
        "w_out": w_out[:, :D].T,
        "b_out": np.asarray(L0_xattn_b_out).reshape(128, 1),
        "gate_w": np.asarray(L0_ffn_gate_w).T,
        "gate_b": np.repeat(np.asarray(L0_ffn_gate_b)[None, :], B, axis=0),
        "expert_w": np.asarray(L0_ffn_expert_w).transpose(2, 0, 1),
        "expert_b": np.asarray(L0_ffn_expert_b).T,
        "consts": constants(),
    }
    arrays = {k: np.ascontiguousarray(v) for k, v in arrays.items()}
    nc = bacc.Bacc("TRN2", target_bir_lowering=False, num_devices=1)
    ins = {k: nc.dram_tensor(f"in_{k}", v.shape, mybir.dt.from_np(v.dtype), kind="ExternalInput").ap()
           for k, v in arrays.items()}
    out = nc.dram_tensor("out", (T, B, D), F32, kind="ExternalOutput").ap()
    xattn_moe(nc, **ins, out=out)
    got = run(nc, [{f"in_{k}": v for k, v in arrays.items()}], core_ids=[0]).results[0]["out"]
    return np.ascontiguousarray(np.asarray(got).transpose(1, 0, 2))
```
